# Optimizing a Trainium2 kernel written in Bass

```python
import numpy as np
import jax
import jax.numpy as jnp

def _softmax(x, axis=-1):
    return jax.nn.softmax(x, axis=axis)

def _gelu(x):
    return jax.nn.gelu(x, approximate=True)

def _silu(x):
    return jax.nn.silu(x)

def _sigmoid(x):
    return jax.nn.sigmoid(x)

def _layernorm(x, axis=-1, eps=1e-05):
    m = jnp.mean(x, axis=axis, keepdims=True)
    v = jnp.var(x, axis=axis, keepdims=True)
    return (x - m) / jnp.sqrt(v + eps)

def _scatter_add(tgt, idx, src, axis=0):
    return tgt.at[idx].add(src)

def _segment_sum(src, seg, n):
    return jax.ops.segment_sum(src, seg, n)
kernel_name = 'mk_decoder_preln_d2_seqx_r8_4fe9ef'

def setup_inputs(seed: int=0):
    np.random.seed(seed)
    _w = jnp.asarray

    def _rec_inputs():
        import jax
        import jax.numpy as jnp
        _rk = jax.random.key(seed)
        x = -0.0002928 + 1 * jax.random.normal(jax.random.fold_in(_rk, 1), (16, 128, 256), jnp.float32)
        _lenS = 128 - jax.random.randint(jax.random.fold_in(_rk, 7), (16,), 0, max(1, 128 // 4) + 1, jnp.int32)
        _lenS2 = 128 - jax.random.randint(jax.random.fold_in(_rk, 8), (16,), 0, max(1, 128 // 4) + 1, jnp.int32)
        _ctx_2048P = jax.random.normal(jax.random.fold_in(_rk, 11), (16, 16, 256), jnp.float32)
        _ctx_2048c = jax.random.dirichlet(jax.random.fold_in(_rk, 511), 0.3 * jnp.ones((16,), jnp.float32), (16, 128))
        _ctx_2048t = jnp.einsum('bsk,bkd->bsd', _ctx_2048c, _ctx_2048P)
        _ctx_2048t = _ctx_2048t * jax.lax.rsqrt(jnp.mean(jnp.square(_ctx_2048t)) + 1e-12) * 0.953939
        ctx_2048 = -1.39393e-06 + 0.999914 * (_ctx_2048t + 0.3 * jax.random.normal(jax.random.fold_in(_rk, 611), (16, 128, 256), jnp.float32))
        _validS = jnp.arange(128)[None, :] < _lenS[:, None]
        _validS2 = jnp.arange(128)[None, :] < _lenS2[:, None]
        _causal = jnp.tril(jnp.ones((128, 128), dtype=bool))
        mask_Bx1x2048_fk1 = jnp.where(jnp.ones((16, 1, 256), dtype=bool), 1.0, 0.0).astype(jnp.float32)
        mask_BxS2_if1 = jnp.where(jnp.ones((16, 128), dtype=bool), 1, 0).astype(jnp.int32)
        return (x, ctx_2048, mask_Bx1x2048_fk1, mask_BxS2_if1)
    x, ctx_2048, mask_Bx1x2048_fk1, mask_BxS2_if1 = _rec_inputs()

    def _L0_attn_setup():
        import jax, jax.numpy as jnp
        import numpy as np
        from jax import lax
        B, T, D = (2, 128, 256)
        H, DK, DV = (16, 128, 128)
        K_CONV = 4

        def _causal_dwconv(y, w, b):
            yc = y.transpose(0, 2, 1)
            out = lax.conv_general_dilated(yc, w, (1,), [(w.shape[-1] - 1, 0)], feature_group_count=yc.shape[1], dimension_numbers=('NCH', 'OIH', 'NCH'))
            return (out + b[None, :, None]).transpose(0, 2, 1)

        def _recurrence(q, k, v, a, beta):

            def step(S, xs):
                q_t, k_t, v_t, a_t, b_t = xs
                Sk = jnp.einsum('bhvk,bhk->bhv', S, k_t)
                S = a_t[..., None] * S - (b_t[..., None] * (Sk - v_t))[..., None] * k_t[:, :, None, :]
                o_t = jnp.einsum('bhvk,bhk->bhv', S, q_t)
                return (S, o_t)
            tfirst = lambda u: jnp.moveaxis(u, 1, 0)
            S0 = jnp.zeros((q.shape[0], q.shape[2], v.shape[3], q.shape[3]), q.dtype)
            _, o = lax.scan(step, S0, (tfirst(q), tfirst(k), tfirst(v), tfirst(a), tfirst(beta)))
            return jnp.moveaxis(o, 0, 1)

        def _forward(x, Wq, Wk, Wv, Wa, ba, Wb, bb, conv_q_w, conv_q_b, conv_k_w, conv_k_b, conv_v_w, conv_v_b, Wg, ln_g, ln_b, Wo):
            B_, T_, _ = x.shape
            q = jax.nn.silu(_causal_dwconv(x @ Wq.T, conv_q_w, conv_q_b))
            k = jax.nn.silu(_causal_dwconv(x @ Wk.T, conv_k_w, conv_k_b))
            v = jax.nn.silu(_causal_dwconv(x @ Wv.T, conv_v_w, conv_v_b))
            q = q.reshape(B_, T_, H, DK)
            k = k.reshape(B_, T_, H, DK) * DK ** (-0.5)
            v = v.reshape(B_, T_, H, DV)
            a = jax.nn.sigmoid(x @ Wa.T + ba).reshape(B_, T_, H, DV)
            beta = jax.nn.sigmoid(x @ Wb.T + bb)
            o = _recurrence(q, k, v, a, beta)
            mu = o.mean(-1, keepdims=True)
            var = ((o - mu) ** 2).mean(-1, keepdims=True)
            o = (o - mu) * lax.rsqrt(var + 1e-05) * ln_g + ln_b
            g = jax.nn.sigmoid(x @ Wg.T).reshape(B_, T_, H, DV)
            o = (o * g).reshape(B_, T_, H * DV)
            return o @ Wo.T
        key = jax.random.key(seed)
        ks = jax.random.split(key, 12)
        s = 0.02
        w = lambda k, shape: jax.random.normal(k, shape, jnp.float32) * s
        return {'x': jax.random.normal(ks[0], (B, T, D), jnp.float32), 'Wq': w(ks[1], (H * DK, D)), 'Wk': w(ks[2], (H * DK, D)), 'Wv': w(ks[3], (H * DV, D)), 'Wa': w(ks[4], (H * DV, D)), 'ba': jnp.zeros((H * DV,), jnp.float32), 'Wb': w(ks[5], (H, D)), 'bb': jnp.zeros((H,), jnp.float32), 'conv_q_w': w(ks[6], (H * DK, 1, K_CONV)), 'conv_q_b': jnp.zeros((H * DK,), jnp.float32), 'conv_k_w': w(ks[7], (H * DK, 1, K_CONV)), 'conv_k_b': jnp.zeros((H * DK,), jnp.float32), 'conv_v_w': w(ks[8], (H * DV, 1, K_CONV)), 'conv_v_b': jnp.zeros((H * DV,), jnp.float32), 'Wg': w(ks[9], (H * DV, D)), 'ln_g': jnp.ones((DV,), jnp.float32), 'ln_b': jnp.zeros((DV,), jnp.float32), 'Wo': w(ks[10], (D, H * DV))}
    _L0_attn_all = _L0_attn_setup()
    _L0_attn_in = {k: v for k, v in _L0_attn_all.items() if k in ('Wq', 'Wk', 'Wv', 'Wa', 'ba', 'Wb', 'bb', 'conv_q_w', 'conv_q_b', 'conv_k_w', 'conv_k_b', 'conv_v_w', 'conv_v_b', 'Wg', 'ln_g', 'ln_b', 'Wo')}
    del _L0_attn_all

    def _L0_xattn_setup():
        import math
        import jax, jax.numpy as jnp
        import numpy as np
        SIZE = 128
        HEADS = 16
        HEAD_DIM = SIZE // HEADS
        B, T, S = (2, 256, 256)
        NEG = 1000000.0
        key = jax.random.key(seed)
        ks = jax.random.split(key, 10)
        target = jax.random.normal(ks[0], (B, SIZE, T), dtype=jnp.float32)
        source = jax.random.normal(ks[1], (B, SIZE, S), dtype=jnp.float32)
        target_mask = (jax.random.uniform(ks[2], (B, 1, T)) > 0.1).astype(jnp.float32)
        source_mask = (jax.random.uniform(ks[3], (B, 1, S)) > 0.1).astype(jnp.float32)
        scale = 1.0 / math.sqrt(SIZE)
        Wq = jax.random.normal(ks[4], (SIZE, SIZE), dtype=jnp.float32) * scale
        Wk = jax.random.normal(ks[5], (SIZE, SIZE), dtype=jnp.float32) * scale
        Wv = jax.random.normal(ks[6], (SIZE, SIZE), dtype=jnp.float32) * scale
        bq = jax.random.normal(ks[7], (SIZE,), dtype=jnp.float32) * 0.01
        bk = jax.random.normal(ks[8], (SIZE,), dtype=jnp.float32) * 0.01
        bv = jax.random.normal(ks[9], (SIZE,), dtype=jnp.float32) * 0.01
        return {'target': target, 'source': source, 'target_mask': target_mask, 'source_mask': source_mask, 'Wq': Wq, 'bq': bq, 'Wk': Wk, 'bk': bk, 'Wv': Wv, 'bv': bv}
    _L0_xattn_all = _L0_xattn_setup()
    _L0_xattn_in = {k: v for k, v in _L0_xattn_all.items() if k in ('Wq', 'bq', 'Wk', 'bk', 'Wv', 'bv')}
    del _L0_xattn_all

    def _L0_ffn_setup():
        import jax, jax.numpy as jnp
        import numpy as np
        BLOCK_SIZE = 32
        HIDDEN_SIZE = 256
        MLP_DIM = 2048
        NVFP4_LUT = jnp.array([0.0, 0.5, 1.0, 1.5, 2.0, 3.0, 4.0, 6.0, 0.0, -0.5, -1.0, -1.5, -2.0, -3.0, -4.0, -6.0], dtype=jnp.float32)

        def dequant_nvfp4(W_packed, scales, block=BLOCK_SIZE):
            N = W_packed.shape[0]
            low = W_packed & 15
            high = W_packed >> 4 & 15
            idx = jnp.stack([low, high], axis=-1).reshape(N, -1)
            vals = NVFP4_LUT[idx]
            K = vals.shape[1]
            vals = vals.reshape(N, K // block, block) * scales[:, :, None]
            return vals.reshape(N, K)
        key = jax.random.key(seed)
        ks = jax.random.split(key, 7)
        x = jax.random.normal(ks[0], (4, 32, HIDDEN_SIZE), dtype=jnp.float32)
        gate_W_packed = jax.random.randint(ks[1], (MLP_DIM, HIDDEN_SIZE // 2), 0, 32, dtype=jnp.int32)
        gate_scales = jax.random.uniform(ks[2], (MLP_DIM, HIDDEN_SIZE // BLOCK_SIZE), dtype=jnp.float32) * 0.1 + 0.001
        up_W_packed = jax.random.randint(ks[3], (MLP_DIM, HIDDEN_SIZE // 2), 0, 32, dtype=jnp.int32)
        up_scales = jax.random.uniform(ks[4], (MLP_DIM, HIDDEN_SIZE // BLOCK_SIZE), dtype=jnp.float32) * 0.1 + 0.001
        down_W_packed = jax.random.randint(ks[5], (HIDDEN_SIZE, MLP_DIM // 2), 0, 32, dtype=jnp.int32)
        down_scales = jax.random.uniform(ks[6], (HIDDEN_SIZE, MLP_DIM // BLOCK_SIZE), dtype=jnp.float32) * 0.1 + 0.001
        return {'x': x, 'gate_W_packed': gate_W_packed, 'gate_scales': gate_scales, 'up_W_packed': up_W_packed, 'up_scales': up_scales, 'down_W_packed': down_W_packed, 'down_scales': down_scales}
    _L0_ffn_all = _L0_ffn_setup()
    _L0_ffn_in = {k: v for k, v in _L0_ffn_all.items() if k in ('gate_W_packed', 'gate_scales', 'up_W_packed', 'up_scales', 'down_W_packed', 'down_scales')}
    del _L0_ffn_all

    def _L1_attn_setup():
        import jax, jax.numpy as jnp
        import numpy as np
        B, T, C, H = (2, 256, 256, 16)
        HD = C // H
        BASE = 10000.0

        def _rope_tables(seq_len, d):
            p = jnp.arange(d // 2, dtype=jnp.float32)
            theta = jnp.power(BASE, -2.0 ** p / d)
            pos = jnp.arange(1, seq_len + 1, dtype=jnp.float32)[:, None]
            c = pos * theta
            ang = jnp.concatenate([c, c], axis=-1)
            return (jnp.cos(ang), jnp.sin(ang))

        def _rope(x):
            d = x.shape[-1]
            cos, sin = _rope_tables(x.shape[-2], d)
            half = d // 2
            x_rot = jnp.concatenate([-x[..., half:], x[..., :half]], axis=-1)
            return x * cos + x_rot * sin
        key = jax.random.key(seed)
        k1, k2, k3 = jax.random.split(key, 3)
        x = jax.random.normal(k1, (B, T, C), dtype=jnp.float32)
        Wqkv = jax.random.normal(k2, (3 * C, C), dtype=jnp.float32) * 0.02
        bqkv = jnp.zeros((3 * C,), dtype=jnp.float32)
        Wo = jax.random.normal(k3, (C, C), dtype=jnp.float32) * 0.02
        bo = jnp.zeros((C,), dtype=jnp.float32)
        return {'x': x, 'Wqkv': Wqkv, 'bqkv': bqkv, 'Wo': Wo, 'bo': bo}
    _L1_attn_all = _L1_attn_setup()
    _L1_attn_in = {k: v for k, v in _L1_attn_all.items() if k in ('Wqkv', 'bqkv', 'Wo', 'bo')}
    del _L1_attn_all

    def _L1_xattn_setup():
        import jax, jax.numpy as jnp
        import numpy as np
        D_MODEL = 256
        N_HEADS = 32
        N_GROUPS = 8
        HEAD_DIM = D_MODEL // N_HEADS
        BATCH, SEQ = (2, 128)
        NEG_INF = float('-inf')
        key = jax.random.key(seed)
        ks = jax.random.split(key, 9)
        s = 0.02
        return {'Q': jax.random.normal(ks[0], (BATCH, SEQ, D_MODEL), jnp.float32), 'K': jax.random.normal(ks[1], (BATCH, SEQ, D_MODEL), jnp.float32), 'V': jax.random.normal(ks[2], (BATCH, SEQ, D_MODEL), jnp.float32), 'attention_mask': jnp.ones((BATCH, SEQ), jnp.int32), 'w_q': jax.random.normal(ks[3], (D_MODEL, D_MODEL), jnp.float32) * s, 'w_k': jax.random.normal(ks[4], (HEAD_DIM * N_GROUPS, D_MODEL), jnp.float32) * s, 'w_v': jax.random.normal(ks[5], (HEAD_DIM * N_GROUPS, D_MODEL), jnp.float32) * s, 'w_o': jax.random.normal(ks[6], (D_MODEL, D_MODEL), jnp.float32) * s, 'b_o': jnp.zeros((D_MODEL,), jnp.float32)}
    _L1_xattn_all = _L1_xattn_setup()
    _L1_xattn_in = {k: v for k, v in _L1_xattn_all.items() if k in ('w_q', 'w_k', 'w_v', 'w_o', 'b_o')}
    del _L1_xattn_all

    def _L1_ffn_setup():
        import jax, jax.numpy as jnp
        import numpy as np
        B, S, H = (2, 256, 256)
        E, K = (16, 4)
        I_MOE, I_SH = (176, 704)
        key = jax.random.key(seed)
        ks = jax.random.split(key, 9)

        def w(k, shape, fan_in):
            return jax.random.normal(k, shape, jnp.float32) * fan_in ** (-0.5)
        return {'hidden_states': jax.random.normal(ks[0], (B, S, H), jnp.float32), 'router_w': w(ks[1], (E, H), H), 'w_gate': w(ks[2], (E, H, I_MOE), H), 'w_up': w(ks[3], (E, H, I_MOE), H), 'w_down': w(ks[4], (E, I_MOE, H), I_MOE), 'sh_gate': w(ks[5], (H, I_SH), H), 'sh_up': w(ks[6], (H, I_SH), H), 'sh_down': w(ks[7], (I_SH, H), I_SH), 'sh_gate_w': w(ks[8], (H, 1), H)}
    _L1_ffn_all = _L1_ffn_setup()
    _L1_ffn_in = {k: v for k, v in _L1_ffn_all.items() if k in ('router_w', 'w_gate', 'w_up', 'w_down', 'sh_gate', 'sh_up', 'sh_down', 'sh_gate_w')}
    del _L1_ffn_all
    return {'x': x, 'ctx_2048': ctx_2048, 'mask_Bx1x2048_fk1': mask_Bx1x2048_fk1, 'mask_BxS2_if1': mask_BxS2_if1, 'L0_attn_Wq': _L0_attn_in['Wq'], 'L0_attn_Wk': _L0_attn_in['Wk'], 'L0_attn_Wv': _L0_attn_in['Wv'], 'L0_attn_Wa': _L0_attn_in['Wa'], 'L0_attn_ba': _L0_attn_in['ba'], 'L0_attn_Wb': _L0_attn_in['Wb'], 'L0_attn_bb': _L0_attn_in['bb'], 'L0_attn_conv_q_w': _L0_attn_in['conv_q_w'], 'L0_attn_conv_q_b': _L0_attn_in['conv_q_b'], 'L0_attn_conv_k_w': _L0_attn_in['conv_k_w'], 'L0_attn_conv_k_b': _L0_attn_in['conv_k_b'], 'L0_attn_conv_v_w': _L0_attn_in['conv_v_w'], 'L0_attn_conv_v_b': _L0_attn_in['conv_v_b'], 'L0_attn_Wg': _L0_attn_in['Wg'], 'L0_attn_ln_g': _L0_attn_in['ln_g'], 'L0_attn_ln_b': _L0_attn_in['ln_b'], 'L0_attn_Wo': _L0_attn_in['Wo'], 'L0_xattn_Wq': _L0_xattn_in['Wq'], 'L0_xattn_bq': _L0_xattn_in['bq'], 'L0_xattn_Wk': _L0_xattn_in['Wk'], 'L0_xattn_bk': _L0_xattn_in['bk'], 'L0_xattn_Wv': _L0_xattn_in['Wv'], 'L0_xattn_bv': _L0_xattn_in['bv'], 'L0_ffn_gate_W_packed': _L0_ffn_in['gate_W_packed'], 'L0_ffn_gate_scales': _L0_ffn_in['gate_scales'], 'L0_ffn_up_W_packed': _L0_ffn_in['up_W_packed'], 'L0_ffn_up_scales': _L0_ffn_in['up_scales'], 'L0_ffn_down_W_packed': _L0_ffn_in['down_W_packed'], 'L0_ffn_down_scales': _L0_ffn_in['down_scales'], 'L1_attn_Wqkv': _L1_attn_in['Wqkv'], 'L1_attn_bqkv': _L1_attn_in['bqkv'], 'L1_attn_Wo': _L1_attn_in['Wo'], 'L1_attn_bo': _L1_attn_in['bo'], 'L1_xattn_w_q': _L1_xattn_in['w_q'], 'L1_xattn_w_k': _L1_xattn_in['w_k'], 'L1_xattn_w_v': _L1_xattn_in['w_v'], 'L1_xattn_w_o': _L1_xattn_in['w_o'], 'L1_xattn_b_o': _L1_xattn_in['b_o'], 'L1_ffn_router_w': _L1_ffn_in['router_w'], 'L1_ffn_w_gate': _L1_ffn_in['w_gate'], 'L1_ffn_w_up': _L1_ffn_in['w_up'], 'L1_ffn_w_down': _L1_ffn_in['w_down'], 'L1_ffn_sh_gate': _L1_ffn_in['sh_gate'], 'L1_ffn_sh_up': _L1_ffn_in['sh_up'], 'L1_ffn_sh_down': _L1_ffn_in['sh_down'], 'L1_ffn_sh_gate_w': _L1_ffn_in['sh_gate_w']}

def reference(x, ctx_2048, mask_Bx1x2048_fk1, mask_BxS2_if1, L0_attn_Wq, L0_attn_Wk, L0_attn_Wv, L0_attn_Wa, L0_attn_ba, L0_attn_Wb, L0_attn_bb, L0_attn_conv_q_w, L0_attn_conv_q_b, L0_attn_conv_k_w, L0_attn_conv_k_b, L0_attn_conv_v_w, L0_attn_conv_v_b, L0_attn_Wg, L0_attn_ln_g, L0_attn_ln_b, L0_attn_Wo, L0_xattn_Wq, L0_xattn_bq, L0_xattn_Wk, L0_xattn_bk, L0_xattn_Wv, L0_xattn_bv, L0_ffn_gate_W_packed, L0_ffn_gate_scales, L0_ffn_up_W_packed, L0_ffn_up_scales, L0_ffn_down_W_packed, L0_ffn_down_scales, L1_attn_Wqkv, L1_attn_bqkv, L1_attn_Wo, L1_attn_bo, L1_xattn_w_q, L1_xattn_w_k, L1_xattn_w_v, L1_xattn_w_o, L1_xattn_b_o, L1_ffn_router_w, L1_ffn_w_gate, L1_ffn_w_up, L1_ffn_w_down, L1_ffn_sh_gate, L1_ffn_sh_up, L1_ffn_sh_down, L1_ffn_sh_gate_w):
    import jax
    import jax.numpy as jnp

    def _L0_attn_ref(x, Wq, Wk, Wv, Wa, ba, Wb, bb, conv_q_w, conv_q_b, conv_k_w, conv_k_b, conv_v_w, conv_v_b, Wg, ln_g, ln_b, Wo):
        import jax, jax.numpy as jnp
        import numpy as np
        from jax import lax
        B, T, D = (2, 128, 256)
        H, DK, DV = (16, 128, 128)
        K_CONV = 4

        def _causal_dwconv(y, w, b):
            yc = y.transpose(0, 2, 1)
            out = lax.conv_general_dilated(yc, w, (1,), [(w.shape[-1] - 1, 0)], feature_group_count=yc.shape[1], dimension_numbers=('NCH', 'OIH', 'NCH'))
            return (out + b[None, :, None]).transpose(0, 2, 1)

        def _recurrence(q, k, v, a, beta):

            def step(S, xs):
                q_t, k_t, v_t, a_t, b_t = xs
                Sk = jnp.einsum('bhvk,bhk->bhv', S, k_t)
                S = a_t[..., None] * S - (b_t[..., None] * (Sk - v_t))[..., None] * k_t[:, :, None, :]
                o_t = jnp.einsum('bhvk,bhk->bhv', S, q_t)
                return (S, o_t)
            tfirst = lambda u: jnp.moveaxis(u, 1, 0)
            S0 = jnp.zeros((q.shape[0], q.shape[2], v.shape[3], q.shape[3]), q.dtype)
            _, o = lax.scan(step, S0, (tfirst(q), tfirst(k), tfirst(v), tfirst(a), tfirst(beta)))
            return jnp.moveaxis(o, 0, 1)

        def _forward(x, Wq, Wk, Wv, Wa, ba, Wb, bb, conv_q_w, conv_q_b, conv_k_w, conv_k_b, conv_v_w, conv_v_b, Wg, ln_g, ln_b, Wo):
            B_, T_, _ = x.shape
            q = jax.nn.silu(_causal_dwconv(x @ Wq.T, conv_q_w, conv_q_b))
            k = jax.nn.silu(_causal_dwconv(x @ Wk.T, conv_k_w, conv_k_b))
            v = jax.nn.silu(_causal_dwconv(x @ Wv.T, conv_v_w, conv_v_b))
            q = q.reshape(B_, T_, H, DK)
            k = k.reshape(B_, T_, H, DK) * DK ** (-0.5)
            v = v.reshape(B_, T_, H, DV)
            a = jax.nn.sigmoid(x @ Wa.T + ba).reshape(B_, T_, H, DV)
            beta = jax.nn.sigmoid(x @ Wb.T + bb)
            o = _recurrence(q, k, v, a, beta)
            mu = o.mean(-1, keepdims=True)
            var = ((o - mu) ** 2).mean(-1, keepdims=True)
            o = (o - mu) * lax.rsqrt(var + 1e-05) * ln_g + ln_b
            g = jax.nn.sigmoid(x @ Wg.T).reshape(B_, T_, H, DV)
            o = (o * g).reshape(B_, T_, H * DV)
            return o @ Wo.T
        return _forward(x, Wq, Wk, Wv, Wa, ba, Wb, bb, conv_q_w, conv_q_b, conv_k_w, conv_k_b, conv_v_w, conv_v_b, Wg, ln_g, ln_b, Wo)

    def _L0_xattn_ref(target, source, target_mask, source_mask, Wq, bq, Wk, bk, Wv, bv):
        import math
        import jax, jax.numpy as jnp
        import numpy as np
        SIZE = 128
        HEADS = 16
        HEAD_DIM = SIZE // HEADS
        B, T, S = (2, 256, 256)
        NEG = 1000000.0
        b, _, t = target.shape
        s = source.shape[-1]
        q = jnp.einsum('oc,bct->bot', Wq, target) + bq[None, :, None]
        k = jnp.einsum('oc,bcs->bos', Wk, source) + bk[None, :, None]
        v = jnp.einsum('oc,bcs->bos', Wv, source) + bv[None, :, None]
        q = q.reshape(b, HEADS, HEAD_DIM, t)
        k = k.reshape(b, HEADS, HEAD_DIM, s)
        v = v.reshape(b, HEADS, HEAD_DIM, s)
        dot = jnp.einsum('bhdt,bhds->bhts', q, k) / math.sqrt(HEAD_DIM)
        mask = target_mask[:, :, :, None] * source_mask[:, :, None, :]
        dot = mask * dot - (1.0 - mask) * NEG
        amap = jax.nn.softmax(dot, axis=-1) * mask
        out = jnp.einsum('bhts,bhds->bhdt', amap, v)
        return out.reshape(b, HEADS * HEAD_DIM, t)

    def _L0_ffn_ref(x, gate_W_packed, gate_scales, up_W_packed, up_scales, down_W_packed, down_scales):
        import jax, jax.numpy as jnp
        import numpy as np
        BLOCK_SIZE = 32
        HIDDEN_SIZE = 256
        MLP_DIM = 2048
        NVFP4_LUT = jnp.array([0.0, 0.5, 1.0, 1.5, 2.0, 3.0, 4.0, 6.0, 0.0, -0.5, -1.0, -1.5, -2.0, -3.0, -4.0, -6.0], dtype=jnp.float32)

        def dequant_nvfp4(W_packed, scales, block=BLOCK_SIZE):
            N = W_packed.shape[0]
            low = W_packed & 15
            high = W_packed >> 4 & 15
            idx = jnp.stack([low, high], axis=-1).reshape(N, -1)
            vals = NVFP4_LUT[idx]
            K = vals.shape[1]
            vals = vals.reshape(N, K // block, block) * scales[:, :, None]
            return vals.reshape(N, K)
        B, S, H = x.shape
        xt = x.reshape(B * S, H)
        Wg = dequant_nvfp4(gate_W_packed, gate_scales)
        Wu = dequant_nvfp4(up_W_packed, up_scales)
        Wd = dequant_nvfp4(down_W_packed, down_scales)
        gate = jnp.einsum('th,nh->tn', xt, Wg)
        up = jnp.einsum('th,nh->tn', xt, Wu)
        gelu = jnp.tanh(0.7978845608028654 * (gate + 0.044715 * gate ** 3)) * gate * 0.5 + gate * 0.5
        inter = gelu * up
        out = jnp.einsum('tn,hn->th', inter, Wd)
        return out.reshape(B, S, H)

    def _L1_attn_ref(x, Wqkv, bqkv, Wo, bo):
        import jax, jax.numpy as jnp
        import numpy as np
        B, T, C, H = (2, 256, 256, 16)
        HD = C // H
        BASE = 10000.0

        def _rope_tables(seq_len, d):
            p = jnp.arange(d // 2, dtype=jnp.float32)
            theta = jnp.power(BASE, -2.0 ** p / d)
            pos = jnp.arange(1, seq_len + 1, dtype=jnp.float32)[:, None]
            c = pos * theta
            ang = jnp.concatenate([c, c], axis=-1)
            return (jnp.cos(ang), jnp.sin(ang))

        def _rope(x):
            d = x.shape[-1]
            cos, sin = _rope_tables(x.shape[-2], d)
            half = d // 2
            x_rot = jnp.concatenate([-x[..., half:], x[..., :half]], axis=-1)
            return x * cos + x_rot * sin
        b, t, c = x.shape
        qkv = x @ Wqkv.T + bqkv
        q, k, v = jnp.split(qkv, 3, axis=-1)

        def to_heads(z):
            return z.reshape(b, t, H, HD).transpose(0, 2, 1, 3)
        q, k, v = (to_heads(q), to_heads(k), to_heads(v))
        q = _rope(q)
        k = _rope(k)
        scale = 1.0 / jnp.sqrt(jnp.float32(HD))
        att = jnp.einsum('bhqd,bhkd->bhqk', q, k) * scale
        causal = jnp.tril(jnp.ones((t, t), dtype=bool))
        att = jnp.where(causal, att, -jnp.inf)
        att = jax.nn.softmax(att, axis=-1)
        y = jnp.einsum('bhqk,bhkd->bhqd', att, v)
        y = y.transpose(0, 2, 1, 3).reshape(b, t, c)
        y = y @ Wo.T + bo
        return y

    def _L1_xattn_ref(Q, K, V, attention_mask, w_q, w_k, w_v, w_o, b_o):
        import jax, jax.numpy as jnp
        import numpy as np
        D_MODEL = 256
        N_HEADS = 32
        N_GROUPS = 8
        HEAD_DIM = D_MODEL // N_HEADS
        BATCH, SEQ = (2, 128)
        NEG_INF = float('-inf')
        B, S, D = Q.shape
        G, HG, HD = (N_GROUPS, N_HEADS // N_GROUPS, HEAD_DIM)
        q = (Q @ w_q.T).reshape(B, S, G, HG, HD)
        k = (K @ w_k.T).reshape(B, S, G, HD)
        v = (V @ w_v.T).reshape(B, S, G, HD)
        scale = jnp.sqrt(jnp.float32(HD))
        scores = jnp.einsum('bnghd,bmgd->bnghm', q, k) / scale
        pad = (attention_mask == 0)[:, None, None, None, :]
        scores = jnp.where(pad, NEG_INF, scores)
        causal = jnp.tril(jnp.ones((S, S), bool))[None, :, None, None, :]
        scores = jnp.where(causal, scores, NEG_INF)
        attn = jax.nn.softmax(scores, axis=-1)
        out = jnp.einsum('bnghm,bmgd->bnghd', attn, v).reshape(B, S, D)
        return out @ w_o.T + b_o

    def _L1_ffn_ref(hidden_states, router_w, w_gate, w_up, w_down, sh_gate, sh_up, sh_down, sh_gate_w):
        import jax, jax.numpy as jnp
        import numpy as np
        B, S, H = (2, 256, 256)
        E, K = (16, 4)
        I_MOE, I_SH = (176, 704)
        orig = hidden_states.shape
        h = hidden_states.reshape(-1, orig[-1])
        N = h.shape[0]
        logits = h @ router_w.T
        probs = jax.nn.softmax(logits.astype(jnp.float32), axis=-1)
        top_vals, top_idx = jax.lax.top_k(probs, K)
        top_vals = top_vals / jnp.maximum(top_vals.sum(-1, keepdims=True), 1e-09)
        top_vals = top_vals.astype(h.dtype)
        comb = jnp.zeros((N, E), h.dtype).at[jnp.arange(N)[:, None], top_idx].add(top_vals)
        g = jnp.einsum('nh,ehi->eni', h, w_gate)
        u = jnp.einsum('nh,ehi->eni', h, w_up)
        y = jnp.einsum('eni,eih->enh', jax.nn.silu(g) * u, w_down)
        routed = jnp.einsum('enh,ne->nh', y, comb)
        shared = jax.nn.silu(h @ sh_gate) * (h @ sh_up) @ sh_down
        sg = jax.nn.sigmoid(h @ sh_gate_w)
        return (routed + sg * shared).reshape(orig)
    x = x + _L0_attn_ref(_layernorm(x, axis=-1), L0_attn_Wq, L0_attn_Wk, L0_attn_Wv, L0_attn_Wa, L0_attn_ba, L0_attn_Wb, L0_attn_bb, L0_attn_conv_q_w, L0_attn_conv_q_b, L0_attn_conv_k_w, L0_attn_conv_k_b, L0_attn_conv_v_w, L0_attn_conv_v_b, L0_attn_Wg, L0_attn_ln_g, L0_attn_ln_b, L0_attn_Wo)
    x = x + _L0_xattn_ref(_layernorm(x, axis=-1), ctx_2048, mask_Bx1x2048_fk1, mask_Bx1x2048_fk1, L0_xattn_Wq, L0_xattn_bq, L0_xattn_Wk, L0_xattn_bk, L0_xattn_Wv, L0_xattn_bv)
    x = x + _L0_ffn_ref(_layernorm(x, axis=-1), L0_ffn_gate_W_packed, L0_ffn_gate_scales, L0_ffn_up_W_packed, L0_ffn_up_scales, L0_ffn_down_W_packed, L0_ffn_down_scales)
    x = x + _L1_attn_ref(_layernorm(x, axis=-1), L1_attn_Wqkv, L1_attn_bqkv, L1_attn_Wo, L1_attn_bo)
    x = x + _L1_xattn_ref(_layernorm(x, axis=-1), ctx_2048, ctx_2048, mask_BxS2_if1, L1_xattn_w_q, L1_xattn_w_k, L1_xattn_w_v, L1_xattn_w_o, L1_xattn_b_o)
    x = x + _L1_ffn_ref(_layernorm(x, axis=-1), L1_ffn_router_w, L1_ffn_w_gate, L1_ffn_w_up, L1_ffn_w_down, L1_ffn_sh_gate, L1_ffn_sh_up, L1_ffn_sh_down, L1_ffn_sh_gate_w)
    return x

_drawn_inputs = setup_inputs


def setup_inputs(seed=0):
    import zlib

    import numpy as np

    out = dict(_drawn_inputs(seed))
    spreads = {'L0_attn_ba': (0.0, 0.8),
     'L0_attn_bb': (0.0, 0.8),
     'L0_attn_conv_q_b': (0.0, 0.316),
     'L0_attn_conv_k_b': (0.0, 0.313),
     'L0_attn_conv_v_b': (0.0, 0.313),
     'L0_attn_ln_g': (1.0, 0.6),
     'L0_attn_ln_b': (0.0, 0.1),
     'L1_attn_bqkv': (0.0, 0.8),
     'L1_attn_bo': (0.0, 0.8),
     'L1_xattn_b_o': (0.0, 0.8)}
    factors = {'L0_attn_Wq': 8.0,
     'L0_attn_Wk': 8.0,
     'L0_attn_Wv': 8.0,
     'L0_attn_Wa': 8.0,
     'L0_attn_Wb': 8.0,
     'L0_attn_conv_q_w': 8.0,
     'L0_attn_conv_k_w': 8.0,
     'L0_attn_conv_v_w': 8.0,
     'L0_attn_Wg': 4.89,
     'L0_xattn_bq': 31.457,
     'L0_xattn_bk': 64.0,
     'L0_xattn_bv': 64.0,
     'L1_attn_Wqkv': 8.0,
     'L1_attn_Wo': 8.0,
     'L1_xattn_w_q': 8.0,
     'L1_xattn_w_k': 8.0,
     'L1_xattn_w_v': 8.0,
     'L1_xattn_w_o': 8.0,
     'L1_ffn_router_w': 2.858,
     'L1_ffn_w_gate': 2.72,
     'L1_ffn_sh_gate': 2.811,
     'L1_ffn_sh_gate_w': 6.933}
    for name, (base, spread) in spreads.items():
        noise = np.random.default_rng([zlib.crc32(name.encode()), seed]).standard_normal(out[name].shape)
        drawn = base * np.exp(spread * noise) if base else spread * noise
        out[name] = jnp.asarray(drawn.astype(out[name].dtype))
    for name, factor in factors.items():
        out[name] = (out[name] * factor).astype(out[name].dtype)
    return out
```

```python
from contextlib import ExitStack

import numpy as np

import concourse.bass as bass
from concourse import mybir

STAGES = (0, 1, 2, 3, 4, 5)

F32 = mybir.dt.float32
I32 = mybir.dt.int32
ALU = mybir.AluOpType
ACT = mybir.ActivationFunctionType
AX = mybir.AxisListType.X

B, T, D = 16, 128, 256
P = 128
KT = D // P
BANK = 512
EPS = 1e-5
MASKED = -1.0e30


class Steps:

    def __init__(self, eng, sem, per_turn=0):
        self.eng, self.sem, self.per_turn, self.k, self.base = eng, sem, per_turn, 0, 0

    def turn(self, n):
        self.base, self.k = n * self.per_turn, 0

    def did(self, ins):
        ins.then_inc(self.sem, 1)
        self.k += 1
        return ins

    def wait(self):
        self.eng.wait_ge(self.sem, self.base + self.k)

    def end(self):
        assert self.k == self.per_turn, (self.k, self.per_turn)


class Section:

    def __init__(self, nc, stack, prefix):
        self.nc, self.stack, self.prefix, self.sems = nc, stack, prefix, []

    def sb(self, name, shape, dt=F32):
        return self.stack.enter_context(self.nc.sbuf_tensor(f"{self.prefix}_{name}", shape, dt))

    def sem(self, name):
        self.sems.append(self.stack.enter_context(self.nc.semaphore(f"{self.prefix}_{name}")))
        return self.sems[-1]

    def close(self):
        with self.nc.Block() as block:

            @block.gpsimd
            def _(pool):
                for sem in self.sems:
                    pool.sem_clear(sem)


def norm_stats(nc, g, prefix):
    with ExitStack() as st:
        s = Section(nc, st, prefix)
        stats = s.sb("stats", [P, B, 6])
        var_root = s.sb("var_root", [P, B])
        stats_done, aggregated = s.sem("stats_done"), s.sem("aggregated")
        rooted, inverted = s.sem("rooted"), s.sem("inverted")
        with nc.Block() as block:

            @block.vector
            def _(dve):
                with dve.Fori(0, B) as b:
                    dve.bn_stats(stats[:, bass.ds(b, 1), :], g.x[:, bass.ds(b, 1), :]).then_inc(stats_done, 1)
                dve.wait_ge(stats_done, B)
                for b in range(B):
                    dve.bn_aggr(g.mean_var[:, b, :], stats[:, b, :]).then_inc(aggregated, 1)
                dve.wait_ge(rooted, 1)
                dve.reciprocal(g.rstd[:, :], var_root[:, :]).then_inc(inverted, 1)
                dve.wait_ge(inverted, 1)

            @block.scalar
            def _(act):
                act.wait_ge(aggregated, B)
                act.activation(var_root[:, :], g.mean_var[:, :, 1], ACT.Sqrt, bias=g.eps[:, 0:1]).then_inc(rooted, 1)
        s.close()


def normalize(dve, g, out, n):
    return dve.tensor_scalar(out, g.x[:, bass.ds(n, 1), :], g.mean_var[:, bass.ds(n, 1), 0],
                             g.rstd[:, bass.ds(n, 1)], ALU.subtract, ALU.mult)


def bcast(ap, axis, count):
    shape = list(ap.shape)
    return ap.unsqueeze(axis).broadcast_to(shape[:axis] + [count] + shape[axis:])


def causal_attention(nc, g, prefix, heads, hd, rope, kv_from_ctx, w):
    per_block = 32 // hd
    per_tile = P // hd
    unit_heads = 4
    units = heads // unit_heads
    halves = 2 if rope else 1
    kv_heads = heads if not kv_from_ctx else heads // per_block
    scale = float(hd) ** -0.5
    dve_steps_a_turn = 1 + (2 if rope else 0) + units + 2 * 1 + 1
    if per_block == 2:
        unit_blocks = [[(0, j), (1, j)] for j in range(4)]
    else:
        unit_blocks = [[(t, j)] for t in range(KT) for j in range(4)]

    with ExitStack() as st:
        s = Section(nc, st, prefix)
        wq = s.sb("wq", [P, KT, halves * D])
        wk = s.sb("wk", [P, KT, halves * D])
        wv = s.sb("wv", [P, KT, kv_heads * hd])
        wo = s.sb("wo", [P, KT, D])
        bias_rows = s.sb("bias_rows", [1, 2 * halves * D + 2 * D])
        cos_sin = s.sb("cos_sin", [P, 2, T])
        head_rows = s.sb("head_rows", [P, per_block])
        causal = s.sb("causal", [P, T])
        mask = s.sb("mask", [P, T])
        pad_int = s.sb("pad_int", [P, B, T], I32)
        pad = s.sb("pad", [P, B, T])
        xn = s.sb("xn", [P, D])
        xnT = s.sb("xnT", [P, KT, T])
        ctxT = s.sb("ctxT", [P, KT, T])
        rope_a = s.sb("rope_a", [P, 2, KT, T])
        rope_b = s.sb("rope_b", [P, 2, KT, T])
        qT = s.sb("qT", [P, KT, T])
        kT = s.sb("kT", [P, KT, T])
        k_spread = s.sb("k_spread", [P, KT, per_block, T])
        v_one = s.sb("v_one", [P, kv_heads, hd + 1])
        probs = s.sb("probs", [P, 2, unit_heads, T])
        peak = s.sb("peak", [P, 2, unit_heads])
        probsT = s.sb("probsT", [P, 2, unit_heads, T])
        recip = s.sb("recip", [P, heads])
        y = s.sb("y", [P, D])
        yT = s.sb("yT", [P, KT, T])

        loaded, ctx_loaded = s.sem("loaded"), s.sem("ctx_loaded")
        ones_set, pad_made, mask_made = s.sem("ones_set"), s.sem("pad_made"), s.sem("mask_made")
        normed, xnT_psum, xnT_done = s.sem("normed"), s.sem("xnT_psum"), s.sem("xnT_done")
        projected, v_done = s.sem("projected"), s.sem("v_done")
        roped, q_done, k_summed, k_done = s.sem("roped"), s.sem("q_done"), s.sem("k_summed"), s.sem("k_done")
        scored, scaled, peaked, shifted = s.sem("scored"), s.sem("scaled"), s.sem("peaked"), s.sem("shifted")
        expd, turned, turned_out = s.sem("expd"), s.sem("turned"), s.sem("turned_out")
        weighed, inverted, y_done = s.sem("weighed"), s.sem("inverted"), s.sem("y_done")
        y_turned, yT_done, out_psum, added = s.sem("y_turned"), s.sem("yT_done"), s.sem("out_psum"), s.sem("added")

        px, pq, pk = g.banks[0], g.banks[1], g.banks[2]
        p_scores = [g.banks[3], g.banks[4]]
        p_turned = [g.banks[5], g.banks[6]]
        p_av = g.banks[7]
        av = p_av[:, 0:heads * (hd + 1)].rearrange("p (h e) -> p h e", e=hd + 1)
        n_loads = 7 + (3 if rope else 0) + (1 if kv_from_ctx else 0) - (0 if rope else 0)

        with nc.Block() as block:

            @block.sync
            def _(sp):
                loads = [(wq, w["wq"]), (wk, w["wk"]), (wv, w["wv"]), (wo, w["wo"]),
                         (head_rows, w["head_rows"]), (causal, w["causal"]), (bias_rows, w["bias_rows"])]
                for dst, src in loads:
                    sp.dma_start(dst[:], src).then_inc(loaded, 16)
                if rope:
                    sp.dma_start(cos_sin[:], w["cos_sin"]).then_inc(loaded, 16)
                if kv_from_ctx:
                    sp.dma_start(pad_int[:], w["pad"].partition_broadcast(P)).then_inc(loaded, 16)
                    with sp.Fori(0, B) as n:
                        sp.wait_ge(added, n + 1)
                        sp.dma_start(ctxT[:, :, :], w["ctxT"][:, :, bass.ds(n, 1), :]).then_inc(ctx_loaded, 16)
                    sp.wait_ge(ctx_loaded, 16 * B)

            all_loads = 16 * 8

            @block.vector
            def _(dve):
                dve.sem_inc(added, 1)
                dve.memset(v_one[:, :, hd:hd + 1], 1.0).then_inc(ones_set, 1)
                dve.wait_ge(loaded, all_loads)
                if kv_from_ctx:
                    dve.tensor_scalar(pad[:, :, :], pad_int[:, :, :], 0, MASKED, ALU.is_equal, ALU.mult)\
                       .then_inc(pad_made, 1)
                with dve.Fori(0, B) as n:
                    dve.wait_ge(added, n + 1)
                    normalize(dve, g, xn[:, :], n).then_inc(normed, 1)
                    dve.wait_ge(projected, 2 * n + 1)
                    if rope:
                        for c, bank in enumerate((pq, pk)):
                            src = bank[:, :].rearrange("p (f c t) -> p f c t", f=2, c=KT)
                            dve.tensor_tensor(rope_a[:, c], src[:, 0], bcast(cos_sin[:, 0, :], 1, KT), ALU.mult)
                            dve.tensor_tensor(rope_b[:, c], src[:, 1], bcast(cos_sin[:, 1, :], 1, KT), ALU.mult)\
                               .then_inc(roped, 1)
                        dve.wait_ge(k_summed, n + 1)
                        k_rows = kT[:, :, :]
                    else:
                        k_rows = pk[:, 0:D].rearrange("p (c t) -> p c t", c=KT)
                    for c in range(KT):
                        ins = dve.tensor_tensor(k_spread[:, c], bcast(k_rows[:, c, :], 1, per_block),
                                                bcast(head_rows[:, :], 2, T), ALU.mult)
                    ins.then_inc(k_done, 1)
                    for u in range(units):
                        dve.wait_ge(scored, n * units + u + 1)
                        if u == 0 and kv_from_ctx:
                            dve.wait_ge(mask_made, n + 1)
                        if u >= 2:
                            dve.wait_ge(turned, n * units + u - 1)
                        m = mask if kv_from_ctx else causal
                        dve.scalar_tensor_tensor(probs[:, u % 2], p_scores[u % 2][:, :].rearrange("p (h t) -> p h t", t=T),
                                                 scale, bcast(m[:, :], 1, unit_heads), ALU.mult, ALU.add)\
                           .then_inc(scaled, 1)
                        dve.wait_ge(scaled, n * units + u + 1)
                        dve.tensor_reduce(peak[:, u % 2], probs[:, u % 2], AX, ALU.max).then_inc(peaked, 1)
                    dve.wait_ge(weighed, n * units + units)
                    dve.reciprocal(recip[:, :], av[:, :, hd]).then_inc(inverted, 1)
                    dve.wait_ge(inverted, n + 1)
                    dve.tensor_tensor(y[:, :].rearrange("p (h e) -> p h e", e=hd), av[:, :, 0:hd],
                                      bcast(recip[:, :], 2, hd), ALU.mult).then_inc(y_done, 1)
                    dve.wait_ge(out_psum, n + 1)
                    dve.tensor_tensor(g.x[:, bass.ds(n, 1), :], g.x[:, bass.ds(n, 1), :], pq[:, 0:D], ALU.add)\
                       .then_inc(added, 1)

            @block.gpsimd
            def _(pool):
                if kv_from_ctx:
                    pool.wait_ge(loaded, all_loads)
                    pool.wait_ge(pad_made, 1)
                with pool.Fori(0, B) as n:
                    if kv_from_ctx:
                        pool.wait_ge(normed, n + 1)
                        pool.tensor_tensor(mask[:, :], causal[:, :], pad[:, bass.ds(n, 1), :], ALU.add)\
                            .then_inc(mask_made, 1)
                    if rope:
                        pool.wait_ge(roped, 2 * n + 1)
                        pool.tensor_tensor(qT[:, :, :], rope_a[:, 0], rope_b[:, 0], ALU.add).then_inc(q_done, 1)
                        pool.wait_ge(roped, 2 * n + 2)
                        pool.tensor_tensor(kT[:, :, :], rope_a[:, 1], rope_b[:, 1], ALU.add).then_inc(k_summed, 1)
                    for u in range(units):
                        pool.wait_ge(peaked, n * units + u + 1)
                        pool.tensor_tensor(probs[:, u % 2], probs[:, u % 2], bcast(peak[:, u % 2], 2, T),
                                           ALU.subtract).then_inc(shifted, 1)

            @block.scalar
            def _(act):
                with act.Fori(0, B) as n:
                    act.wait_ge(xnT_psum, n + 1)
                    act.copy(xnT[:, :, :], px[:, 0:D].rearrange("p (c t) -> p c t", c=KT)).then_inc(xnT_done, 1)
                    act.wait_ge(projected, 2 * n + 2)
                    if not rope:
                        act.copy(qT[:, :, :], pq[:, 0:D].rearrange("p (c t) -> p c t", c=KT)).then_inc(q_done, 1)
                    act.wait_ge(ones_set, 1)
                    act.copy(v_one[:, :, 0:hd], px[:, D:D + kv_heads * hd].rearrange("p (h e) -> p h e", e=hd))\
                       .then_inc(v_done, 1)

                    def turn_out(u):
                        act.wait_ge(turned, n * units + u + 1)
                        if u >= 2:
                            act.wait_ge(weighed, n * units + u - 1)
                        act.copy(probsT[:, u % 2], p_turned[u % 2][:, :].rearrange("p (h t) -> p h t", t=T))\
                           .then_inc(turned_out, 1)

                    for u in range(units):
                        act.wait_ge(shifted, n * units + u + 1)
                        act.activation(probs[:, u % 2], probs[:, u % 2], ACT.Exp).then_inc(expd, 1)
                        if u >= 1:
                            turn_out(u - 1)
                    turn_out(units - 1)
                    act.wait_ge(y_turned, n + 1)
                    act.copy(yT[:, :, :], px[:, 0:D].rearrange("p (c t) -> p c t", c=KT)).then_inc(yT_done, 1)

            @block.tensor
            def _(pe):
                pe.wait_ge(loaded, all_loads)
                q_bias, k_bias = 0, halves * D
                v_bias, o_bias = 2 * halves * D, 2 * halves * D + D
                with pe.Fori(0, B) as n:
                    pe.wait_ge(normed, n + 1)
                    for c in range(KT):
                        ins = pe.transpose(px[:, c * T:(c + 1) * T], xn[:, c * P:(c + 1) * P], g.ident[:, :])
                    ins.then_inc(xnT_psum, 1)
                    pe.wait_ge(xnT_done, n + 1)
                    if kv_from_ctx:
                        pe.wait_ge(ctx_loaded, 16 * n + 16)
                    kv_src = ctxT if kv_from_ctx else xnT
                    for bank, wt, off, src in ((pq, wq, q_bias, xnT), (pk, wk, k_bias, kv_src)):
                        for f in range(halves * KT):
                            o = bank[:, f * T:(f + 1) * T]
                            for c in range(KT):
                                ins = pe.matmul(o, wt[:, c, f * P:(f + 1) * P], src[:, c, :],
                                                start=(c == 0), stop=(c == KT - 1 and not rope))
                            if rope:
                                ins = pe.matmul(o, bias_rows[0:1, off + f * P:off + (f + 1) * P], g.ones[0:1, 0:T],
                                                start=False, stop=True)
                    ins.then_inc(projected, 1)
                    o = px[:, D:D + kv_heads * hd]
                    for c in range(KT):
                        ins = pe.matmul(o, kv_src[:, c, :], wv[:, c, :], start=(c == 0), stop=(c == KT - 1 and not rope))
                    if rope:
                        ins = pe.matmul(o, g.ones[0:1, 0:T], bias_rows[0:1, v_bias:v_bias + D], start=False, stop=True)
                    ins.then_inc(projected, 1)

                    def scores(u):
                        if u == 0:
                            pe.wait_ge(q_done, n + 1)
                            pe.wait_ge(k_done, n + 1)
                        if u >= 2:
                            pe.wait_ge(peaked, n * units + u - 1)
                        width = BANK // len(unit_blocks[u])
                        for i, (c, j) in enumerate(unit_blocks[u]):
                            rows = slice(32 * j, 32 * j + 32)
                            ins = pe.matmul(p_scores[u % 2][:, i * width:(i + 1) * width], qT[rows, c, :],
                                            k_spread[rows, c, :, :], start=True, stop=True)
                        ins.then_inc(scored, 1)

                    def turn(u):
                        pe.wait_ge(expd, n * units + u + 1)
                        if u >= 2:
                            pe.wait_ge(turned_out, n * units + u - 1)
                        for h in range(unit_heads):
                            ins = pe.transpose(p_turned[u % 2][:, h * T:(h + 1) * T], probs[:, u % 2, h, :], g.ident[:, :])
                        ins.then_inc(turned, 1)

                    def weigh(u):
                        if u == 0:
                            pe.wait_ge(v_done, n + 1)
                        pe.wait_ge(turned_out, n * units + u + 1)
                        unit = [c * per_tile + j * per_block + k for c, j in unit_blocks[u] for k in range(per_block)]
                        for i, h in enumerate(unit):
                            kv = h // per_block if kv_from_ctx else h
                            ins = pe.matmul(av[:, h, :], probsT[:, u % 2, i, :], v_one[:, kv, :], start=True, stop=True)
                        ins.then_inc(weighed, 1)

                    scores(0)
                    scores(1)
                    turn(0)
                    for u in range(1, units):
                        if u + 1 < units:
                            scores(u + 1)
                        turn(u)
                        weigh(u - 1)
                    weigh(units - 1)
                    pe.wait_ge(y_done, n + 1)
                    for c in range(KT):
                        ins = pe.transpose(px[:, c * T:(c + 1) * T], y[:, c * P:(c + 1) * P], g.ident[:, :])
                    ins.then_inc(y_turned, 1)
                    pe.wait_ge(yT_done, n + 1)
                    for c in range(KT):
                        pe.matmul(pq[:, 0:D], yT[:, c, :], wo[:, c, :], start=(c == 0), stop=False)
                    pe.matmul(pq[:, 0:D], g.ones[0:1, 0:T], bias_rows[0:1, o_bias:o_bias + D],
                              start=False, stop=True).then_inc(out_psum, 1)
        s.close()


def layer1_attention(nc, g):
    norm_stats(nc, g, "n3")
    w = dict(wq=g.dram["a1_wq"], wk=g.dram["a1_wk"], wv=g.dram["a1_wv"], wo=g.dram["a1_wo"],
             head_rows=g.dram["head_rows16"], causal=g.dram["causal"], bias_rows=g.dram["a1_bias"],
             cos_sin=g.dram["cos_sin"])
    causal_attention(nc, g, "a1", 16, 16, True, False, w)


def layer1_cross(nc, g):
    norm_stats(nc, g, "n4")
    w = dict(wq=g.dram["c1_wq"], wk=g.dram["c1_wk"], wv=g.dram["c1_wv"], wo=g.dram["c1_wo"],
             head_rows=g.dram["head_rows8"], causal=g.dram["causal"], bias_rows=g.dram["c1_bias"],
             pad=g.dram["mask_BxS2_if1"], ctxT=g.dram["ctxT"])
    causal_attention(nc, g, "c1", 32, 8, False, True, w)



class Count:

    def __init__(self, sem, per_turn, start=0, by=1):
        self.sem, self.per_turn, self.start, self.by = sem, per_turn, start, by

    def wait(self, eng, n, k):
        assert k + self.start > 0
        eng.wait_ge(self.sem, n * (self.per_turn * self.by) + (k + self.start) * self.by)

    def rise(self, ins):
        return ins.then_inc(self.sem, self.by)

    def open(self, eng):
        eng.sem_inc(self.sem, self.start * self.by)


def layer0_attention(nc, g):
    norm_stats(nc, g, "n0")
    H, HD = 16, P
    TURNS = B // 2
    N2 = 2 * T
    CH = 16
    NC = T // CH
    PERIOD, LAG = 24, 12
    W_COLS, N_SCALARS = KT * 641, 17
    KIND_K, KIND_Q, KIND_KT, KIND_QT = range(4)
    k_scale = float(HD) ** -0.5

    with ExitStack() as st:
        s = Section(nc, st, "a0")
        wbuf = [s.sb(f"wbuf{p}", [P, W_COLS + N_SCALARS]) for p in range(2)]
        xn = s.sb("xn", [P, 2, D])
        xnT = s.sb("xnT", [P, KT, N2])
        raw = [s.sb(f"raw{p}", [P, 3, 2, T + 3]) for p in range(2)]
        acc = [s.sb(f"acc{p}", [P, 3, 2, T]) for p in range(2)]
        beta = [s.sb(f"beta{p}", [P, 2, T]) for p in range(2)]
        q_h = [s.sb(f"q{p}", [P, 2, T]) for p in range(2)]
        k_h = [s.sb(f"k{p}", [P, 2, T]) for p in range(2)]
        kb_h = [s.sb(f"kb{p}", [P, 2, T]) for p in range(2)]
        vb = s.sb("vb", [P, 2, H, T])
        decay = s.sb("decay", [P, 2, H, T])
        gate = s.sb("gate", [P, 2, H, T])
        dots = s.sb("dots", [P, 2, H, 4, T])
        past = s.sb("past", [P, 2, H, T])
        live = s.sb("live", [P, 2, 2, H, CH + 1])
        pastT = s.sb("pastT", [P, 2, 4, P])
        y0 = s.sb("y0", [P, 2, H, 2 * CH])
        prod = s.sb("prod", [P, 2, 2, H * CH])
        sums = s.sb("sums", [P, 2, 2, 2, H])
        ye = s.sb("ye", [P, 2, 2, H, 2])
        rest = s.sb("rest", [P, 2, 2, H])
        ln = s.sb("ln", [P, 2])
        mean_ones = s.sb("mean_ones", [P, P])
        wo = dots[:, 0, 0:8, :, :].rearrange("p a b c -> p (a b c)").rearrange("p (h d) -> p h d", h=H)
        square = [past[:, 0, 0:4, :], past[:, 0, 4:8, :]]
        root = [past[:, 0, 8:12, :], past[:, 0, 12:16, :]]

        def sig_of(p):
            return raw[p][:, :, :, 3:]

        def counts(name, per_turn, start=0, by=1):
            return Count(s.sem(name), per_turn, start, by)

        w_loaded = [counts(f"w_loaded{p}", H // 2, by=16) for p in range(2)]
        ln_loaded, wo_loaded = s.sem("ln_loaded"), counts("wo_loaded", 1, by=16)
        set_up = s.sem("set_up")
        normed, xnT_psum, xnT_done = counts("normed", 2), counts("xnT_psum", 1), counts("xnT_done", 1)
        projected, raw_done, gates_done = counts("projected", H), counts("raw_done", H), counts("gates_done", H, 2)
        conv_step, sig_done = counts("conv_step", 4 * H), counts("sig_done", H, 2)
        k_done, qkv_done = counts("k_done", H), counts("qkv_done", H, 2)
        pool_step = counts("pool_step", H)
        dotted, dots_out = [counts(f"dotted{b}", H) for b in range(2)], [counts(f"dots_out{b}", H, 1) for b in range(2)]
        spread = [counts(f"spread{b}", NC * CH) for b in range(2)]
        multiplied = [counts(f"multiplied{b}", NC * CH) for b in range(2)]
        summed = [counts(f"summed{b}", NC * CH) for b in range(2)]
        u_done = [counts(f"u_done{b}", NC * CH) for b in range(2)]
        ye_done = [counts(f"ye_done{b}", NC * CH) for b in range(2)]
        rest_done = [counts(f"rest_done{b}", NC * CH) for b in range(2)]
        decayed = [counts(f"decayed{b}", NC * CH) for b in range(2)]
        o_done = [counts(f"o_done{b}", NC * CH) for b in range(2)]
        y0_zero = counts("y0_zero", 1)
        past_done = [counts(f"past_done{b}", 4 * (NC - 1)) for b in range(2)]
        past_turned, past_out = counts("past_turned", 8 * (NC - 1)), counts("past_out", 8 * (NC - 1))
        past_used = counts("past_used", 8 * (NC - 1))
        y0_out = [counts(f"y0_out{b}", NC - 1) for b in range(2)]
        mean_psum, centred, squared = counts("mean_psum", 8), counts("centred", 8), counts("squared", 8)
        var_psum, rooted, inverted = counts("var_psum", 8), counts("rooted", 8), counts("inverted", 8)
        normal, gated = counts("normal", 8), counts("gated", 8)
        out_psum, added = counts("out_psum", 2), counts("added", 2, 2)

        p_proj = [[g.banks[3 * p + i] for i in range(3)] for p in range(2)]
        p_dots = [g.banks[6], g.banks[7]]
        p_spread = [[g.banks[0], g.banks[1]], [g.banks[2], g.banks[3]]]
        p_past, p_y0 = [g.banks[4], g.banks[5]], [g.banks[6], g.banks[7]]
        p_mean, p_var, p_out = [g.banks[0], g.banks[1]], [g.banks[2], g.banks[3]], [g.banks[4], g.banks[5]]

        def slots():
            for slot in range(PERIOD * NC + LAG):
                steps, parts = [], []
                for b in range(2):
                    m, r = divmod(slot - LAG * b, PERIOD)
                    if 0 <= m < NC and r <= CH:
                        steps.append((b, m, r))
                    elif 0 <= m < NC - 1:
                        parts.append((b, m, r - CH - 1))
                yield slot, steps, parts

        def scalar(p, k):
            return wbuf[p][:, W_COLS + k:W_COLS + k + 1]

        with nc.Block() as block:

            @block.sync
            def _(sp):
                sp.dma_start(ln[:, :], g.dram["a0_ln"]).then_inc(ln_loaded, 16)
                with sp.Fori(0, TURNS) as n:
                    for h in range(H):
                        sig_done.wait(sp, n, h - 1)
                        w_loaded[h % 2].rise(sp.dma_start(wbuf[h % 2][:, :], g.dram["a0_w"][h]))
                    for b in range(2):
                        spread[b].wait(sp, n, NC * CH)
                    wo_loaded.rise(sp.dma_start(wo, g.dram["a0_wo"]))
                for p in range(2):
                    sp.wait_ge(w_loaded[p].sem, 16 * TURNS * H // 2)
                sp.wait_ge(wo_loaded.sem, 16 * TURNS)

            @block.vector
            def _(dve):
                added.open(dve)
                for p in range(2):
                    dve.memset(raw[p][:, :, :, 0:3], 0.0).then_inc(set_up, 1)
                dve.memset(mean_ones[:, :], 1.0 / HD).then_inc(set_up, 1)
                dve.memset(past[:, :, :, :], 0.0).then_inc(set_up, 1)
                dve.wait_ge(set_up, 4)
                dve.wait_ge(ln_loaded, 16)

                def convolve(n, h):
                    p = h % 2
                    raw_done.wait(dve, n, h + 1)
                    qkv_done.wait(dve, n, h - 1)
                    for c in range(3):
                        ins = dve.tensor_scalar(acc[p][:, c], raw[p][:, c, :, 3:], scalar(p, 4 * c + 3), scalar(p, 12 + c),
                                                ALU.mult, ALU.add)
                    conv_step.rise(ins)
                    for j in (2, 1, 0):
                        conv_step.wait(dve, n, 4 * h + 3 - j)
                        for c in range(3):
                            ins = dve.scalar_tensor_tensor(acc[p][:, c], raw[p][:, c, :, j:j + T], scalar(p, 4 * c + j),
                                                           acc[p][:, c], ALU.mult, ALU.add)
                        conv_step.rise(ins)

                def make_k(n, h):
                    p = h % 2
                    sig_done.wait(dve, n, h + 1)
                    if h >= 2:
                        dots_out[1].wait(dve, n, h - 1)
                    k_done.rise(dve.scalar_tensor_tensor(k_h[p][:, :, :], acc[p][:, 1], k_scale, sig_of(p)[:, 1], ALU.mult, ALU.mult))

                def step(n, b, m, j):
                    e = m * CH + j
                    first = 0 if j < CH else 1

                    def multiply():
                        if j == 0:
                            return
                        spread[b].wait(dve, n, e)
                        decayed[b].wait(dve, n, e)
                        u_done[b].wait(dve, n, e)
                        view = prod[:, b, :, 0:H * j].rearrange("p c (h i) -> p c h i", i=j)
                        rows = p_spread[b][j % 2][:, 0:2 * H * j].rearrange("p (c h i) -> p c h i", c=2, i=j)
                        us = bcast(live[:, b, j % 2, :, 1:j + 1], 1, 2)
                        multiplied[b].rise(dve.tensor_tensor(view[:, first:], us[:, first:], rows[:, first:], ALU.mult))

                    def total():
                        if j == 0:
                            return
                        multiplied[b].wait(dve, n, e)
                        if j >= 3:
                            o_done[b].wait(dve, n, e - 2)
                        view = prod[:, b, :, 0:H * j].rearrange("p c (h i) -> p c h i", i=j)
                        summed[b].rise(dve.tensor_reduce(sums[:, b, j % 2, first:], view[:, first:], AX, ALU.add))

                    def update():
                        if j == CH:
                            return
                        rest_done[b].wait(dve, n, e + 1)
                        new = live[:, b, (j + 1) % 2, :, j + 1]
                        if j == 0:
                            ins = dve.tensor_copy(new, rest[:, b, 0])
                        else:
                            summed[b].wait(dve, n, e)
                            ins = dve.tensor_tensor(new, rest[:, b, j % 2], sums[:, b, j % 2, 0], ALU.subtract)
                        u_done[b].rise(ins)

                    return multiply, total, update

                with dve.Fori(0, TURNS) as n:
                    added.wait(dve, n, 0)
                    for b in range(2):
                        normed.rise(normalize(dve, g, xn[:, b, :], 2 * n + b))
                    y0_zero.rise(dve.memset(y0[:, :, :, :], 0.0))
                    for h in range(H):
                        if h >= 1:
                            make_k(n, h - 1)
                        convolve(n, h)
                    make_k(n, H - 1)
                    for _, steps, _ in slots():
                        parts = [step(n, *x) for x in steps]
                        for i in range(3):
                            for x in parts:
                                x[i]()
                    def group(i):
                        b, q = divmod(i, 4)
                        return slice(4 * q, 4 * q + 4), b

                    def centre(i):
                        hs, b = group(i)
                        mean_psum.wait(dve, n, i + 1)
                        centred.rise(dve.tensor_tensor(vb[:, b, hs, :], vb[:, b, hs, :],
                                                       p_mean[i % 2][:, :].rearrange("p (h t) -> p h t", t=T), ALU.subtract))

                    def finish(i):
                        hs, b = group(i)
                        o = vb[:, b, hs, :]
                        rooted.wait(dve, n, i + 1)
                        inverted.rise(dve.reciprocal(root[i % 2], root[i % 2]))
                        inverted.wait(dve, n, i + 1)
                        normal.rise(dve.scalar_tensor_tensor(o, o, ln[:, 0:1], root[i % 2], ALU.mult, ALU.mult))
                        normal.wait(dve, n, i + 1)
                        gated.rise(dve.scalar_tensor_tensor(o, o, ln[:, 1:2], gate[:, b, hs, :], ALU.add, ALU.mult))

                    centre(0)
                    centre(1)
                    for i in range(8):
                        if i + 2 < 8:
                            centre(i + 2)
                        finish(i)
                    for b in range(2):
                        out_psum.wait(dve, n, b + 1)
                        added.rise(dve.tensor_tensor(g.x[:, bass.ds(2 * n + b, 1), :], g.x[:, bass.ds(2 * n + b, 1), :],
                                                     p_out[b][:, 0:D], ALU.add))

            @block.gpsimd
            def _(pool):
                qkv_done.open(pool)
                with pool.Fori(0, TURNS) as n:
                    normed.wait(pool, n, 2)
                    for h in range(H):
                        p = h % 2
                        sig_done.wait(pool, n, h + 1)
                        if h >= 2:
                            dots_out[1].wait(pool, n, h - 1)
                        pool.tensor_tensor(q_h[p][:, :, :], acc[p][:, 0], sig_of(p)[:, 0], ALU.mult)
                        pool_step.rise(pool.tensor_tensor(acc[p][:, 2], acc[p][:, 2], sig_of(p)[:, 2], ALU.mult))
                        pool_step.wait(pool, n, h + 1)
                        pool.tensor_tensor(vb[:, :, h, :], acc[p][:, 2], beta[p][:, :, :], ALU.mult)
                        k_done.wait(pool, n, h + 1)
                        qkv_done.rise(pool.tensor_tensor(kb_h[p][:, :, :], k_h[p][:, :, :], beta[p][:, :, :], ALU.mult))

                    def output(b, m, j):
                        summed[b].wait(pool, n, m * CH + j)
                        o_done[b].rise(pool.tensor_tensor(vb[:, b, :, m * CH + j - 1], sums[:, b, j % 2, 1], ye[:, b, j % 2, :, 1], ALU.add))

                    def step(b, m, j):
                        e = m * CH + j
                        now, then = live[:, b, j % 2], live[:, b, (j + 1) % 2]
                        if j == 0:
                            if m == 0:
                                y0_zero.wait(pool, n, 1)
                            else:
                                y0_out[b].wait(pool, n, m)
                            qkv_done.wait(pool, n, H)
                            rest_done[b].rise(pool.tensor_tensor(rest[:, b, 0], vb[:, b, :, e], y0[:, b, :, 0], ALU.subtract))
                            decayed[b].rise(pool.tensor_tensor(then[:, :, 0], decay[:, b, :, e], g.ones[:, 0:H], ALU.mult))
                            return
                        decayed[b].wait(pool, n, e)
                        if e > 2:
                            o_done[b].wait(pool, n, e - 2)
                        ye_done[b].rise(pool.tensor_tensor(ye[:, b, j % 2], bcast(now[:, :, 0], 2, 2),
                                                           y0[:, b, :, j:j + CH:CH - 1], ALU.mult))
                        if j < CH:
                            ye_done[b].wait(pool, n, e)
                            rest_done[b].rise(pool.tensor_tensor(rest[:, b, j % 2], vb[:, b, :, e], ye[:, b, j % 2, :, 0], ALU.subtract))
                            u_done[b].wait(pool, n, e)
                            decayed[b].rise(pool.tensor_tensor(then[:, :, 0:j + 1], now[:, :, 0:j + 1],
                                                               bcast(decay[:, b, :, e], 2, j + 1), ALU.mult))
                        if j >= 2:
                            output(b, m, j - 1)
                        if j == CH:
                            ye_done[b].wait(pool, n, e)
                            output(b, m, CH)

                    def boundary(b, m, part):
                        if part > 3:
                            return
                        hs, t0 = slice(4 * part, 4 * part + 4), m * CH
                        if part == 0:
                            decayed[b].wait(pool, n, t0 + CH)
                            u_done[b].wait(pool, n, t0 + CH)
                        if m > 0:
                            pool.tensor_tensor(past[:, b, hs, 0:t0], past[:, b, hs, 0:t0], bcast(live[:, b, 0, hs, 0], 2, t0), ALU.mult)
                        past_done[b].rise(pool.tensor_tensor(past[:, b, hs, t0:t0 + CH], live[:, b, 0, hs, 1:CH + 1],
                                                             bcast(g.ones[:, 0:CH], 1, 4), ALU.mult))

                    for _, steps, parts in slots():
                        for x in steps:
                            step(*x)
                        for x in parts:
                            boundary(*x)

            @block.scalar
            def _(act):
                gates_done.open(act)
                sig_done.open(act)
                for b in range(2):
                    dots_out[b].open(act)
                act.wait_ge(set_up, 4)
                with act.Fori(0, TURNS) as n:

                    def evacuate(h):
                        p = h % 2
                        projected.wait(act, n, h + 1)
                        if h >= 2:
                            qkv_done.wait(act, n, h - 1)
                        act.copy(raw[p][:, 0:2, :, 3:], p_proj[p][0][:, :].rearrange("p (c b t) -> p c b t", c=2, b=2))
                        raw_done.rise(act.copy(raw[p][:, 2, :, 3:], p_proj[p][1][:, 0:N2].rearrange("p (b t) -> p b t", b=2)))
                        act.activation(decay[:, :, h, :], p_proj[p][1][:, N2:2 * N2].rearrange("p (b t) -> p b t", b=2),
                                       ACT.Sigmoid, bias=scalar(p, 15))
                        act.activation(gate[:, :, h, :], p_proj[p][2][:, 0:N2].rearrange("p (b t) -> p b t", b=2), ACT.Sigmoid)
                        gates_done.rise(act.activation(beta[p][:, :, :], p_proj[p][2][:, N2:2 * N2].rearrange("p (b t) -> p b t", b=2),
                                                       ACT.Sigmoid, bias=scalar(p, 16)))

                    def copy_dots(h):
                        for b in range(2):
                            dotted[b].wait(act, n, h + 1)
                            dots_out[b].rise(act.copy(dots[:, b, h, :, :], p_dots[b][:, :].rearrange("p (c t) -> p c t", c=4)))

                    xnT_psum.wait(act, n, 1)
                    xnT_done.rise(act.copy(xnT[:, :, :], g.banks[6][:, :].rearrange("p (c t) -> p c t", c=KT)))
                    for h in range(H):
                        evacuate(h)
                        if h >= 1:
                            copy_dots(h - 1)
                        conv_step.wait(act, n, 4 * h + 4)
                        for c in range(3):
                            ins = act.activation(sig_of(h % 2)[:, c], acc[h % 2][:, c], ACT.Sigmoid)
                        sig_done.rise(ins)
                    copy_dots(H - 1)

                    def boundary(b, m, part):
                        e = (2 * m + b) * 4
                        if part < 4:
                            past_turned.wait(act, n, e + part + 1)
                            if e + part >= 2:
                                past_used.wait(act, n, e + part - 1)
                            past_out.rise(act.copy(pastT[0:(m + 1) * CH, part % 2], p_past[part % 2][0:(m + 1) * CH, :]
                                                   .rearrange("p (h v) -> p h v", h=4)))
                        if part == 4:
                            past_used.wait(act, n, e + 4)
                            ye_done[b].wait(act, n, (m + 1) * CH)
                            y0_out[b].rise(act.copy(y0[:, b, :, :], p_y0[b][:, :].rearrange("p (h c) -> p h c", h=H)))

                    for _, _, parts in slots():
                        for x in parts:
                            boundary(*x)

                    def square_of(i):
                        b, q = divmod(i, 4)
                        centred.wait(act, n, i + 1)
                        if i >= 2:
                            var_psum.wait(act, n, i - 1)
                        squared.rise(act.activation(square[i % 2], vb[:, b, 4 * q:4 * q + 4, :], ACT.Square))

                    def root_of(i):
                        var_psum.wait(act, n, i + 1)
                        if i >= 2:
                            normal.wait(act, n, i - 1)
                        rooted.rise(act.activation(root[i % 2], p_var[i % 2][:, :].rearrange("p (h t) -> p h t", t=T), ACT.Sqrt,
                                                   bias=g.eps[:, 0:1]))

                    square_of(0)
                    for i in range(8):
                        if i + 1 < 8:
                            square_of(i + 1)
                        root_of(i)

            @block.tensor
            def _(pe):
                pe.wait_ge(set_up, 4)
                with pe.Fori(0, TURNS) as n:

                    def project(h):
                        p = h % 2
                        w_loaded[p].wait(pe, n, h // 2 + 1)
                        gates_done.wait(pe, n, h - 1)
                        w = wbuf[p][:, 0:W_COLS].rearrange("p (c f) -> p c f", c=KT)
                        for i in range(6):
                            o = p_proj[p][i // 2][:, (i % 2) * N2:(i % 2 + 1) * N2]
                            for c in range(KT):
                                lhsT = w[:, c, i * P:(i + 1) * P] if i < 5 else w[:, c, 640:641].broadcast_to([P, P])
                                ins = pe.matmul(o, lhsT, xnT[:, c, :], start=(c == 0), stop=(c == KT - 1))
                        projected.rise(ins)

                    def dot(h):
                        p = h % 2
                        qkv_done.wait(pe, n, h + 1)
                        for b in range(2):
                            dots_out[b].wait(pe, n, h)
                            k, q, kb = k_h[p][:, b, :], q_h[p][:, b, :], kb_h[p][:, b, :]
                            for kind, lhsT, rhs in ((KIND_K, kb, k), (KIND_Q, q, k), (KIND_KT, k, kb), (KIND_QT, k, q)):
                                ins = pe.matmul(p_dots[b][:, kind * T:(kind + 1) * T], lhsT, rhs, start=True, stop=True)
                            dotted[b].rise(ins)

                    def spread_rows(b, m, j):
                        if j == 0:
                            return
                        e = m * CH + j
                        if e == 1:
                            for x in range(2):
                                dots_out[x].wait(pe, n, H)
                        if e > 2:
                            multiplied[b].wait(pe, n, e - 2)
                        t0 = m * CH
                        for kind in (KIND_K, KIND_Q):
                            if kind == KIND_K and j == CH:
                                continue
                            t = t0 + j if kind == KIND_K else t0 + j - 1
                            ins = pe.matmul(p_spread[b][j % 2][:, kind * H * j:(kind + 1) * H * j],
                                            g.ident[:, t:t + 1].broadcast_to([P, P]), dots[:, b, :, kind, t0:t0 + j],
                                            start=True, stop=True)
                        spread[b].rise(ins)

                    def boundary(b, m, part):
                        e = (2 * m + b) * 4
                        k = (m + 1) * CH
                        if part < 4:
                            past_done[b].wait(pe, n, 4 * m + part + 1)
                            if e + part >= 2:
                                past_out.wait(pe, n, e + part - 1)
                            for i in range(4):
                                ins = pe.transpose(p_past[part % 2][:, i * P:(i + 1) * P], past[:, b, 4 * part + i, :], g.ident[:, :])
                            past_turned.rise(ins)
                        if 1 <= part <= 4:
                            q = part - 1
                            past_out.wait(pe, n, e + q + 1)
                            for i in range(4):
                                h = 4 * q + i
                                ins = pe.matmul(p_y0[b][:, h * 2 * CH:(h + 1) * 2 * CH], pastT[0:k, q % 2, i, :],
                                                dots[0:k, b, h, KIND_KT:KIND_QT + 1, k:k + CH], start=True, stop=True)
                            past_used.rise(ins)

                    normed.wait(pe, n, 2)
                    for b in range(2):
                        for c in range(KT):
                            o = c * N2 + b * T
                            ins = pe.transpose(g.banks[6][:, o:o + T], xn[:, b, c * P:(c + 1) * P], g.ident[:, :])
                    xnT_psum.rise(ins)
                    xnT_done.wait(pe, n, 1)
                    project(0)
                    for h in range(1, H):
                        project(h)
                        dot(h - 1)
                    dot(H - 1)

                    all_slots = list(slots())
                    for i, (_, steps, parts) in enumerate(all_slots):
                        if i == 0:
                            for x in steps:
                                spread_rows(*x)
                        if i + 1 < len(all_slots):
                            for x in all_slots[i + 1][1]:
                                spread_rows(*x)
                        for x in parts:
                            boundary(*x)

                    def mean_of(i):
                        b, q = divmod(i, 4)
                        if i == 0:
                            for x in range(2):
                                multiplied[x].wait(pe, n, NC * CH)
                        if i % 4 == 0:
                            o_done[b].wait(pe, n, NC * CH)
                        if i >= 2:
                            centred.wait(pe, n, i - 1)
                        mean_psum.rise(pe.matmul(p_mean[i % 2][:, :], mean_ones[:, :], vb[:, b, 4 * q:4 * q + 4, :], start=True, stop=True))

                    def var_of(i):
                        squared.wait(pe, n, i + 1)
                        if i >= 2:
                            rooted.wait(pe, n, i - 1)
                        var_psum.rise(pe.matmul(p_var[i % 2][:, :], mean_ones[:, :], square[i % 2], start=True, stop=True))

                    mean_of(0)
                    mean_of(1)
                    for i in range(8):
                        if i + 2 < 8:
                            mean_of(i + 2)
                        var_of(i)
                    wo_loaded.wait(pe, n, 1)
                    for b in range(2):
                        for h in range(H):
                            if h % 4 == 0:
                                gated.wait(pe, n, 4 * b + h // 4 + 1)
                            ins = pe.matmul(p_out[b][:, 0:D], vb[:, b, h, :], wo[:, h, :], start=(h == 0), stop=(h == H - 1))
                        out_psum.rise(ins)
        s.close()


def layer0_cross(nc, g):
    norm_stats(nc, g, "n1")
    HEADS, HD, S = 16, 8, D
    PER_BLOCK = 4
    BIG = 1.0e6
    UNITS = [(tt, j, hp) for tt in range(2) for j in range(4) for hp in range(2)]
    NU = len(UNITS)
    scale = float(HD) ** -0.5
    with ExitStack() as st:
        s = Section(nc, st, "c0")
        wq, wk, wv = (s.sb(k, [P, P]) for k in ("wq", "wk", "wv"))
        bias_rows = s.sb("bias_rows", [1, 3 * P])
        head_rows = s.sb("head_rows", [P, PER_BLOCK])
        mask_all = s.sb("mask_all", [P, B, S])
        mask_col = s.sb("mask_col", [P, 2, B])
        mask_big = s.sb("mask_big", [P, 2, B])
        minus_big = s.sb("minus_big", [P, 1])
        pause = s.sb("pause", [P, 2])
        xn = s.sb("xn", [P, D])
        ctx_n = s.sb("ctx_n", [P, 2, D])
        qT = s.sb("qT", [P, D])
        kT = s.sb("kT", [P, S])
        k_spread = s.sb("k_spread", [P, PER_BLOCK, S])
        v_one = s.sb("v_one", [P, 2, HEADS, HD + 1])
        add_mask = s.sb("add_mask", [P, 2, S])
        probs = s.sb("probs", [P, 3, 2, S])
        low = s.sb("low", [P, 3, 2])
        probsT = s.sb("probsT", [P, 2, 2, 2, T])
        recip = s.sb("recip", [P, 2, HEADS])
        y = s.sb("y", [P, 2, P])
        loaded, ctx_loaded = s.sem("loaded"), [s.sem("ctx_loaded0"), s.sem("ctx_loaded1")]
        ctx_used = s.sem("ctx_used")
        ones_set, big_made, add_made = s.sem("ones_set"), s.sem("big_made"), s.sem("add_made")
        normed, projected, q_done, k_masked, k_done = (s.sem(k) for k in ("normed", "projected", "q_done", "k_masked", "k_done"))
        v_done, scored, negated, expd = (s.sem(k) for k in ("v_done", "scored", "negated", "expd"))
        turned, turned_out, weighed = (s.sem(k) for k in ("turned", "turned_out", "weighed"))
        recip_step, y_done, y_turned, added = (s.sem(k) for k in ("recip_step", "y_done", "y_turned", "added"))
        p_qk, p_v, p_av = g.banks[0], g.banks[1], g.banks[2]
        p_scores, p_turned = [g.banks[3], g.banks[4], g.banks[5]], [g.banks[6], g.banks[7]]
        av = p_av[:, 0:2 * HEADS * (HD + 1)].rearrange("p (t h e) -> p t h e", t=2, e=HD + 1)
        LOADS = 16 * 7

        with nc.Block() as block:

            @block.sync
            def _(sp):
                for dst, src in ((wq, "c0_wq"), (wk, "c0_wk"), (wv, "c0_wv"), (bias_rows, "c0_bias"),
                                 (head_rows, "head_rows8"), (mask_col, "c0_mask_col")):
                    sp.dma_start(dst[:], g.dram[src]).then_inc(loaded, 16)
                sp.dma_start(mask_all[:], g.dram["c0_mask"].partition_broadcast(P)).then_inc(loaded, 16)
                with sp.Fori(0, B // 2) as i:
                    for b in range(2):
                        sp.wait_ge(ctx_used, 2 * i + b + 1)
                        sp.dma_start(ctx_n[:, b, :], g.dram["ctx_2048"][bass.ds(2 * i + b, 1), :, :])\
                          .then_inc(ctx_loaded[b], 16)
                for b in range(2):
                    sp.wait_ge(ctx_loaded[b], 16 * B // 2)

            @block.vector
            def _(dve):
                def copy_out(n, u):
                    dve.wait_ge(turned, n * NU + u + 1)
                    if u >= 2:
                        dve.wait_ge(weighed, n * NU + u - 1)
                    dve.tensor_copy(probsT[:, u % 2], p_turned[u % 2][:, :].rearrange("p (h c t) -> p h c t", h=2, c=2))\
                       .then_inc(turned_out, 1)

                dve.sem_inc(added, 1)
                dve.memset(v_one[:, :, :, HD:HD + 1], 1.0).then_inc(ones_set, 1)
                dve.memset(minus_big[:, :], -BIG).then_inc(ones_set, 1)
                dve.wait_ge(loaded, LOADS)
                dve.tensor_scalar(mask_big[:, :, :], mask_col[:, :, :], BIG, None, ALU.mult).then_inc(big_made, 1)
                with dve.Fori(0, B // 2) as i:
                    for b in range(2):
                        n = 2 * i + b
                        dve.wait_ge(added, n + 1)
                        normalize(dve, g, xn[:, :], n).then_inc(normed, 1)
                        dve.wait_ge(projected, 2 * n + 1)
                        dve.scalar_tensor_tensor(qT[:, :], p_qk[:, 0:D], scale, mask_all[:, bass.ds(n, 1), :], ALU.mult,
                                                 ALU.mult).then_inc(q_done, 1)
                        dve.tensor_tensor(kT[:, :], p_qk[:, D:2 * D], mask_all[:, bass.ds(n, 1), :], ALU.mult).then_inc(k_masked, 1)
                        dve.wait_ge(k_masked, n + 1)
                        dve.tensor_tensor(k_spread[:, :, :], bcast(kT[:, :], 1, PER_BLOCK), bcast(head_rows[:, :], 2, S),
                                          ALU.mult).then_inc(k_done, 1)
                        for u, (tt, j, hp) in enumerate(UNITS):
                            dve.wait_ge(scored, n * NU + u + 1)
                            if u == 0:
                                dve.wait_ge(add_made, n + 1)
                            if u >= 2:
                                copy_out(n, u - 2)
                            else:
                                dve.memset(pause[:, u:u + 1], 0.0)
                            for h in range(2):
                                ins = dve.tensor_tensor_reduce(
                                    probs[:, u % 3, h], p_scores[u % 3][:, h * S:(h + 1) * S], add_mask[:, tt, :],
                                    -1.0, 3.0e38, ALU.add, ALU.min, low[:, u % 3, h:h + 1])
                            ins.then_inc(negated, 1)
                        copy_out(n, NU - 2)
                        copy_out(n, NU - 1)
                        dve.wait_ge(weighed, n * NU + NU)
                        dve.reciprocal(recip[:, :, :], av[:, :, :, HD]).then_inc(recip_step, 1)
                        dve.wait_ge(recip_step, 2 * n + 1)
                        dve.tensor_tensor(recip[:, :, :], recip[:, :, :],
                                          bcast(mask_col[:, :, bass.ds(n, 1)].rearrange("p t n -> p (t n)"), 2, HEADS),
                                          ALU.mult).then_inc(recip_step, 1)
                        dve.wait_ge(recip_step, 2 * n + 2)
                        for tt in range(2):
                            ins = dve.tensor_tensor(y[:, tt, :].rearrange("p (h e) -> p h e", e=HD), av[:, tt, :, 0:HD],
                                                    bcast(recip[:, tt, :], 2, HD), ALU.mult)
                        ins.then_inc(y_done, 1)
                        dve.wait_ge(y_turned, n + 1)
                        dve.tensor_tensor(g.x[:, bass.ds(n, 1), :], g.x[:, bass.ds(n, 1), :], p_v[:, 0:D], ALU.add)\
                           .then_inc(added, 1)

            @block.scalar
            def _(act):
                act.wait_ge(ones_set, 2)
                act.wait_ge(big_made, 1)
                act.wait_ge(loaded, LOADS)
                with act.Fori(0, B) as n:
                    act.wait_ge(normed, n + 1)
                    for tt in range(2):
                        ins = act.activation(add_mask[:, tt, :], mask_all[:, bass.ds(n, 1), :], ACT.Identity,
                                             bias=minus_big[:, :], scale=mask_big[:, tt, bass.ds(n, 1)])
                    ins.then_inc(add_made, 1)
                    act.wait_ge(projected, 2 * n + 2)
                    for c in range(2):
                        ins = act.activation(v_one[:, c, :, 0:HD], p_v[:, c * P:(c + 1) * P].rearrange("p (h e) -> p h e", e=HD),
                                             ACT.Copy, scale=mask_col[:, c, bass.ds(n, 1)])
                    ins.then_inc(v_done, 1)
                    for u in range(NU):
                        act.wait_ge(negated, n * NU + u + 1)
                        for h in range(2):
                            ins = act.activation(probs[:, u % 3, h], probs[:, u % 3, h], ACT.Exp,
                                                 bias=low[:, u % 3, h:h + 1], scale=-1.0)
                        ins.then_inc(expd, 1)

            @block.tensor
            def _(pe):
                pe.sem_inc(ctx_used, 2)
                pe.wait_ge(loaded, LOADS)
                with pe.Fori(0, B // 2) as i:
                    for b in range(2):
                        n = 2 * i + b
                        pe.wait_ge(normed, n + 1)
                        pe.matmul(p_qk[:, 0:D], wq[:, :], xn[:, :], start=True, stop=False)
                        pe.matmul(p_qk[:, 0:D], bias_rows[0:1, 0:P], bcast(g.ones[0:1, 0:P], 1, 2), start=False, stop=True)
                        pe.wait_ge(ctx_loaded[b], 16 * i + 16)
                        pe.matmul(p_qk[:, D:2 * D], wk[:, :], ctx_n[:, b, :], start=True, stop=False)
                        pe.matmul(p_qk[:, D:2 * D], bias_rows[0:1, P:2 * P], bcast(g.ones[0:1, 0:P], 1, 2),
                                  start=False, stop=True).then_inc(projected, 1)
                        for c in range(2):
                            o = p_v[:, c * P:(c + 1) * P]
                            ins = pe.matmul(o, ctx_n[:, b, c * P:(c + 1) * P], wv[:, :], start=True, stop=False)
                            ins2 = pe.matmul(o, g.ones[0:1, 0:P], bias_rows[0:1, 2 * P:3 * P], start=False, stop=True)
                        ins.then_inc(ctx_used, 1)
                        ins2.then_inc(projected, 1)

                        def scores(u):
                            tt, j, hp = UNITS[u]
                            if u == 0:
                                pe.wait_ge(q_done, n + 1)
                                pe.wait_ge(k_done, n + 1)
                            if u >= 3:
                                pe.wait_ge(negated, n * NU + u - 2)
                            rows = slice(32 * j, 32 * j + 32)
                            pe.matmul(p_scores[u % 3][:, :], qT[rows, tt * P:(tt + 1) * P], k_spread[rows, 2 * hp:2 * hp + 2, :],
                                      start=True, stop=True).then_inc(scored, 1)

                        def turn(u):
                            pe.wait_ge(expd, n * NU + u + 1)
                            if u >= 2:
                                pe.wait_ge(turned_out, n * NU + u - 1)
                            for h in range(2):
                                for c in range(2):
                                    o = (2 * h + c) * T
                                    ins = pe.transpose(p_turned[u % 2][:, o:o + T], probs[:, u % 3, h, c * P:(c + 1) * P], g.ident[:, :])
                            ins.then_inc(turned, 1)

                        def weigh(u):
                            tt, j, hp = UNITS[u]
                            if u == 0:
                                pe.wait_ge(v_done, n + 1)
                            pe.wait_ge(turned_out, n * NU + u + 1)
                            for h in range(2):
                                head = PER_BLOCK * j + 2 * hp + h
                                for c in range(2):
                                    ins = pe.matmul(av[:, tt, head, :], probsT[:, u % 2, h, c, :], v_one[:, c, head, :],
                                                    start=(c == 0), stop=(c == 1))
                            ins.then_inc(weighed, 1)

                        scores(0)
                        scores(1)
                        turn(0)
                        for u in range(1, NU):
                            if u + 1 < NU:
                                scores(u + 1)
                            turn(u)
                            weigh(u - 1)
                        weigh(NU - 1)
                        pe.wait_ge(y_done, n + 1)
                        for tt in range(2):
                            ins = pe.transpose(p_v[:, tt * P:(tt + 1) * P], y[:, tt, :], g.ident[:, :])
                        ins.then_inc(y_turned, 1)
        s.close()


def gated_mlp(nc, s, g, tiles, act_fn, strided, wg, wu, wd, router):
    n_tok = 2 * T
    turns = B // 2
    xn = s.sb("xn", [P, 2, D])
    xnT = s.sb("xnT", [P, KT, n_tok])
    gated = s.sb("gated", [P, 2, n_tok])
    hidden = s.sb("hidden", [P, 3, n_tok])
    normed, xnT_psum, xnT_done = s.sem("normed"), s.sem("xnT_psum"), s.sem("xnT_done")
    projected, activated, upped = s.sem("projected"), s.sem("activated"), s.sem("upped")
    hidden_done, downed, added = s.sem("hidden_done"), s.sem("downed"), s.sem("added")
    p_turn, p_gu = g.banks[0], [g.banks[1], g.banks[2], g.banks[3]]
    p_weight, p_acc, p_route = [g.banks[4], g.banks[7]], [g.banks[5], g.banks[6]], g.banks[0]
    if router:
        NE = router["experts"] + 1
        wr, expert_rows = router["wr"], router["expert_rows"]
        raw = s.sb("raw", [P, 2, NE])
        top8 = s.sb("top8", [P, 2, 8])
        rest = s.sb("rest", [P, 2, NE - 1])
        stat = s.sb("stat", [P, 4, 2])
        shared_tanh = s.sb("shared_tanh", [P, 2, 1])
        mix = s.sb("mix", [P, 2, NE])
        pause = s.sb("pause", [P, 1])
        combT = s.sb("combT", [NE, n_tok])
        weighted = s.sem("weighted")
        routed_in, route_step = s.sem("routed_in"), s.sem("route_step")
        exp_done, mix_done = s.sem("exp_done"), s.sem("mix_done")
        mix_turned, combT_done = s.sem("mix_turned"), s.sem("combT_done")
        ROUTE_STEPS = 14

    with nc.Block() as block:

        @block.vector
        def _(dve):
            dve.sem_inc(added, 2)
            if router:
                step = Steps(dve, route_step, ROUTE_STEPS)
            with dve.Fori(0, turns) as n:
                dve.wait_ge(added, 2 * n + 2)
                for b in range(2):
                    normalize(dve, g, xn[:, b, :], 2 * n + b).then_inc(normed, 1)
                if router:
                    step.turn(n)
                    dve.wait_ge(routed_in, n + 1)
                    logits = p_route[:, 0:2 * NE].rearrange("p (b e) -> p b e", e=NE)
                    step.did(dve.tensor_reduce(stat[:, 0], logits[:, :, 0:NE - 1], AX, ALU.max))
                    step.wait()
                    step.did(dve.tensor_tensor(raw[:, :, 0:NE - 1], logits[:, :, 0:NE - 1], bcast(stat[:, 0], 2, NE - 1), ALU.subtract))
                    dve.wait_ge(exp_done, n + 1)
                    step.did(dve.tensor_reduce(stat[:, 1], raw[:, :, 0:NE - 1], AX, ALU.add))
                    step.wait()
                    step.did(dve.reciprocal(stat[:, 1], stat[:, 1]))
                    step.wait()
                    step.did(dve.tensor_tensor(raw[:, :, 0:NE - 1], raw[:, :, 0:NE - 1], bcast(stat[:, 1], 2, NE - 1), ALU.mult))
                    step.wait()
                    dve.memset(pause[:, :], 0.0)
                    for b in range(2):
                        ins = dve.max(top8[:, b, :], raw[:, b, 0:NE - 1])
                    step.did(ins)
                    step.wait()
                    step.did(dve.memset(top8[:, :, router["top"]:], -1.0))
                    step.wait()
                    dve.memset(pause[:, :], 0.0)
                    for b in range(2):
                        ins = dve.match_replace(rest[:, b, :], top8[:, b, :], raw[:, b, 0:NE - 1], 0.0)
                    step.did(ins)
                    step.wait()
                    step.did(dve.tensor_tensor(mix[:, :, 0:NE - 1], raw[:, :, 0:NE - 1], rest[:, :, :], ALU.subtract))
                    step.wait()
                    step.did(dve.tensor_reduce(stat[:, 2], mix[:, :, 0:NE - 1], AX, ALU.add))
                    step.wait()
                    step.did(dve.tensor_scalar(stat[:, 2], stat[:, 2], 1e-9, None, ALU.max))
                    step.wait()
                    step.did(dve.reciprocal(stat[:, 3], stat[:, 2]))
                    step.wait()
                    step.did(dve.tensor_tensor(mix[:, :, 0:NE - 1], mix[:, :, 0:NE - 1], bcast(stat[:, 3], 2, NE - 1), ALU.mult))
                    step.did(dve.tensor_scalar(mix[:, :, NE - 1:NE], shared_tanh[:, :, :], 0.5, 0.5, ALU.mult, ALU.add))
                    step.end()
                for t in range(tiles):
                    dve.wait_ge(activated, n * tiles + t + 1)
                    if t >= 3:
                        dve.wait_ge(downed, n * tiles + t - 2)
                    up = p_gu[t % 3][:, n_tok:2 * n_tok]
                    if not router:
                        dve.tensor_tensor(hidden[:, t % 3, :], gated[:, t % 2, :], up, ALU.mult).then_inc(hidden_done, 1)
                        continue
                    dve.tensor_tensor(gated[:, t % 2, :], gated[:, t % 2, :], up, ALU.mult).then_inc(upped, 1)
                    dve.wait_ge(upped, n * tiles + t + 1)
                    dve.wait_ge(weighted, n * tiles + t + 1)
                    dve.tensor_tensor(hidden[:, t % 3, :], gated[:, t % 2, :], p_weight[t % 2][:, 0:n_tok], ALU.mult)\
                       .then_inc(hidden_done, 1)
                dve.wait_ge(downed, n * tiles + tiles)
                for b in range(2):
                    dve.tensor_tensor(g.x[:, bass.ds(2 * n + b, 1), :], g.x[:, bass.ds(2 * n + b, 1), :],
                                      p_acc[b][:, 0:D], ALU.add).then_inc(added, 1)

        @block.scalar
        def _(act):
            with act.Fori(0, turns) as n:
                act.wait_ge(xnT_psum, n + 1)
                act.copy(xnT[:, :, :], p_turn[:, :].rearrange("p (c t) -> p c t", c=KT)).then_inc(xnT_done, 1)
                if router:
                    logits = p_route[:, 0:2 * NE].rearrange("p (b e) -> p b e", e=NE)
                    act.wait_ge(route_step, n * ROUTE_STEPS + 2)
                    act.activation(shared_tanh[:, :, :], logits[:, :, NE - 1:NE], ACT.Tanh, scale=0.5)
                    act.activation(raw[:, :, 0:NE - 1], raw[:, :, 0:NE - 1], ACT.Exp).then_inc(exp_done, 1)
                    act.wait_ge(mix_turned, n + 1)
                    act.copy(combT[:, :], p_route[0:NE, n_tok:2 * n_tok]).then_inc(combT_done, 1)
                for t in range(tiles):
                    act.wait_ge(projected, n * tiles + t + 1)
                    if t >= 2:
                        act.wait_ge(hidden_done, n * tiles + t - 1)
                    act.activation(gated[:, t % 2, :], p_gu[t % 3][:, 0:n_tok], act_fn).then_inc(activated, 1)

        @block.tensor
        def _(pe):
            with pe.Fori(0, turns) as n:
                pe.wait_ge(normed, 2 * n + 2)
                for b in range(2):
                    for c in range(KT):
                        src = xn[:, b, c::2] if strided else xn[:, b, c * P:(c + 1) * P]
                        o = c * n_tok + b * T
                        ins = pe.transpose(p_turn[:, o:o + T], src, g.ident[:, :])
                ins.then_inc(xnT_psum, 1)
                pe.wait_ge(xnT_done, n + 1)
                if router:
                    for b in range(2):
                        for c in range(KT):
                            ins = pe.matmul(p_route[:, b * NE:(b + 1) * NE], xnT[:, c, b * T:(b + 1) * T], wr[:, c, :],
                                            start=(c == 0), stop=(c == KT - 1))
                    ins.then_inc(routed_in, 1)

                def up(t):
                    if t >= 3:
                        pe.wait_ge(hidden_done, n * tiles + t - 2)
                    for w, o in ((wg, 0), (wu, n_tok)):
                        for c in range(KT):
                            ins = pe.matmul(p_gu[t % 3][:, o:o + n_tok], w[:, c, t * P:(t + 1) * P], xnT[:, c, :],
                                            start=(c == 0), stop=(c == KT - 1))
                    ins.then_inc(projected, 1)

                def weight(t):
                    if t >= 2:
                        pe.wait_ge(hidden_done, n * tiles + t - 1)
                    pe.matmul(p_weight[t % 2][:, 0:n_tok], expert_rows[:, t * P:(t + 1) * P], combT[:, :],
                              start=True, stop=True).then_inc(weighted, 1)

                def down(t):
                    pe.wait_ge(hidden_done, n * tiles + t + 1)
                    for b in range(2):
                        ins = pe.matmul(p_acc[b][:, 0:D], hidden[:, t % 3, b * T:(b + 1) * T], wd[:, t, :],
                                        start=(t == 0), stop=(t == tiles - 1))
                    ins.then_inc(downed, 1)

                up(0)
                up(1)
                if router:
                    pe.wait_ge(route_step, (n + 1) * ROUTE_STEPS)
                    for b in range(2):
                        o = n_tok + b * T
                        ins = pe.transpose(p_route[0:NE, o:o + T], mix[:, b, :], g.ident[:, :])
                    ins.then_inc(mix_turned, 1)
                    pe.wait_ge(combT_done, n + 1)
                    weight(0)
                for t in range(1, tiles):
                    if t + 1 < tiles:
                        up(t + 1)
                    if router:
                        weight(t)
                    down(t - 1)
                down(tiles - 1)


def layer1_moe(nc, g):
    norm_stats(nc, g, "n5")
    tiles = g.dram["e1_wg"].shape[-1] // P
    with ExitStack() as st:
        s = Section(nc, st, "e1")
        wg = s.sb("wg", [P, KT, tiles * P])
        wu = s.sb("wu", [P, KT, tiles * P])
        wd = s.sb("wd", [P, tiles, D])
        wr = s.sb("wr", [P, KT, 17])
        expert_rows = s.sb("expert_rows", [17, tiles * P])
        loaded = s.sem("loaded")
        with nc.Block() as block:

            @block.sync
            def _(sp):
                for dst, src in ((wr, "wr"), (wg, "wg"), (wu, "wu"), (wd, "wd"), (expert_rows, "expert_rows")):
                    sp.dma_start(dst[:], g.dram["e1_" + src]).then_inc(loaded, 16)
                sp.wait_ge(loaded, 16 * 5)

        gated_mlp(nc, s, g, tiles, ACT.Silu, False, wg, wu, wd,
                  dict(experts=16, top=4, wr=wr, expert_rows=expert_rows))
        s.close()


def layer0_mlp(nc, g):
    norm_stats(nc, g, "n2")
    F = 2048
    CH = 1024
    with ExitStack() as st:
        s = Section(nc, st, "m0")
        wg = s.sb("wg", [P, KT, F])
        wu = s.sb("wu", [P, KT, F])
        wd = s.sb("wd", [P, F // P, D])
        with ExitStack() as st2:
            q = Section(nc, st2, "m0q")
            codes = q.sb("codes", [P, 3, F], I32)
            scales = q.sb("scales", [P, 3, F])
            m = q.sb("m", [P, 2, CH], I32)
            sign = q.sb("sign", [P, 2, CH], I32)
            over4 = q.sb("over4", [P, 2, CH])
            over6 = q.sb("over6", [P, 2, CH])
            signed_scale = q.sb("signed_scale", [P, 2, CH])
            bias = q.sb("bias", [P, 3])
            loaded, bias_set = [q.sem(f"loaded{k}") for k in range(3)], q.sem("bias_set")
            bits, sloped, sign_done = q.sem("bits"), q.sem("sloped"), q.sem("sign_done")
            scaled, summed, valued, done = q.sem("scaled"), q.sem("summed"), q.sem("valued"), q.sem("done")
            dests = []
            for k in range(3):
                for half in range(F // CH):
                    for par in range(2):
                        cols = slice(half * CH, (half + 1) * CH)
                        if k < 2:
                            out = (wg, wu)[k][:, par, cols]
                        else:
                            per = CH // D
                            out = wd[:, :, :].rearrange("p (j r) d -> p j r d", r=2)[:, half * per:(half + 1) * per, par, :]
                        dests.append((out, k, par, cols))
            with nc.Block() as block:

                @block.sync
                def _(sp):
                    for k in range(3):
                        sp.dma_start(codes[:, k, :], g.dram["m0_codes"][:, k, :]).then_inc(loaded[k], 16)
                        for r in range(8):
                            sp.dma_start(scales[16 * r:16 * r + 16, k, :],
                                         g.dram["m0_scales"][r, k, :].partition_broadcast(16)).then_inc(loaded[k], 16)

                @block.vector
                def _(dve):
                    dve.memset(bias[:, 0:1], -2.0).then_inc(bias_set, 1)
                    dve.memset(bias[:, 1:2], -6.0).then_inc(bias_set, 1)
                    dve.memset(bias[:, 2:3], 1.0).then_inc(bias_set, 1)

                    def split(i):
                        out, k, par, cols = dests[i]
                        dve.wait_ge(loaded[k], 144)
                        if i >= 2:
                            dve.wait_ge(valued, i - 1)
                            dve.wait_ge(sloped, 3 * (i - 1))
                        dve.tensor_scalar(m[:, i % 2], codes[:, k, cols], 4 * par, 7, ALU.logical_shift_right, ALU.bitwise_and)
                        dve.tensor_scalar(sign[:, i % 2], codes[:, k, cols], 4 * par + 3, 1, ALU.logical_shift_right,
                                          ALU.bitwise_and).then_inc(bits, 1)

                    def combine(i):
                        out, k, par, cols = dests[i]
                        dve.wait_ge(sloped, 3 * (i + 1))
                        dve.tensor_tensor(over4[:, i % 2], over4[:, i % 2], over6[:, i % 2], ALU.add).then_inc(summed, 1)
                        dve.wait_ge(summed, i + 1)
                        dve.scalar_tensor_tensor(over6[:, i % 2], m[:, i % 2], 0.5, over4[:, i % 2], ALU.mult, ALU.add)\
                           .then_inc(valued, 1)
                        dve.wait_ge(valued, i + 1)
                        dve.wait_ge(scaled, i + 1)
                        ss, v = signed_scale[:, i % 2], over6[:, i % 2]
                        if k == 2:
                            ss, v = (a.rearrange("p (j d) -> p j d", d=D) for a in (ss, v))
                        dve.tensor_tensor(out, v, ss, ALU.mult).then_inc(done, 1)

                    split(0)
                    for i in range(len(dests)):
                        if i + 1 < len(dests):
                            split(i + 1)
                        combine(i)
                    dve.wait_ge(done, len(dests))

                @block.scalar
                def _(act):
                    act.wait_ge(bias_set, 3)
                    for i in range(len(dests)):
                        act.wait_ge(bits, i + 1)
                        if i >= 2:
                            act.wait_ge(done, i - 1)
                        act.activation(over4[:, i % 2], m[:, i % 2], ACT.Relu, bias=bias[:, 0:1], scale=0.5).then_inc(sloped, 1)
                        act.activation(over6[:, i % 2], m[:, i % 2], ACT.Relu, bias=bias[:, 1:2]).then_inc(sloped, 1)
                        act.activation(signed_scale[:, i % 2], sign[:, i % 2], ACT.Identity, bias=bias[:, 2:3], scale=-2.0)\
                           .then_inc(sloped, 1)

                @block.gpsimd
                def _(pool):
                    for i, (out, k, par, cols) in enumerate(dests):
                        pool.wait_ge(loaded[k], 144)
                        pool.wait_ge(sloped, 3 * (i + 1))
                        pool.tensor_tensor(signed_scale[:, i % 2], signed_scale[:, i % 2], scales[:, k, cols], ALU.mult)\
                            .then_inc(scaled, 1)
            q.close()

        gated_mlp(nc, s, g, F // P, ACT.Gelu_apprx_tanh, True, wg, wu, wd, None)
        s.close()


class Globals:
    pass


def build(nc, dram, out):
    g = Globals()
    g.dram = dram
    with ExitStack() as st:
        s = Section(nc, st, "g")
        g.x = s.sb("x", [P, B, D])
        g.mean_var = s.sb("mean_var", [P, B, 2])
        g.rstd = s.sb("rstd", [P, B])
        g.ident = s.sb("ident", [P, P])
        g.ones = s.sb("ones", [P, P])
        g.eps = s.sb("eps", [P, 1])
        g.banks = [st.enter_context(nc.psum_tensor(f"bank{i}", [P, BANK], F32)) for i in range(8)]
        x_loaded, constants_set, stored = s.sem("x_loaded"), s.sem("constants_set"), s.sem("stored")
        with nc.Block() as block:

            @block.sync
            def _(sp):
                sp.dma_start(g.x[:, :, :], dram["x"].rearrange("b t d -> t b d")).then_inc(x_loaded, 16)
                sp.dma_start(g.ident[:, :], dram["ident"]).then_inc(x_loaded, 16)
                sp.wait_ge(x_loaded, 32)

            @block.vector
            def _(dve):
                dve.memset(g.ones[:, :], 1.0).then_inc(constants_set, 1)
                dve.memset(g.eps[:, :], EPS).then_inc(constants_set, 1)
                dve.wait_ge(constants_set, 2)

        sublayers = (layer0_attention, layer0_cross, layer0_mlp, layer1_attention, layer1_cross, layer1_moe)
        for k in STAGES:
            sublayers[k](nc, g)

        with nc.Block() as block:

            @block.sync
            def _(sp):
                sp.dma_start(out.rearrange("b t d -> t b d"), g.x[:, :, :]).then_inc(stored, 16)
                sp.wait_ge(stored, 16)


def contraction_major(a):
    return np.ascontiguousarray(a.reshape(-1, P, a.shape[-1]).transpose(1, 0, 2))


def constants():
    c = {"ident": np.eye(P, dtype=np.float32)}
    c["causal"] = np.where(np.tril(np.ones((T, T), bool)), 0.0, MASKED).astype(np.float32)
    rows = np.arange(P)
    for hd in (8, 16):
        per_block = 32 // hd
        c[f"head_rows{hd}"] = ((rows[:, None] // hd) % per_block == np.arange(per_block)[None]).astype(np.float32)
    hd = 16
    theta = np.power(np.float32(10000.0), -np.float32(2.0) ** np.arange(hd // 2, dtype=np.float32) / np.float32(hd))
    angle = (np.arange(1, T + 1, dtype=np.float32)[None, :] * theta[:, None].astype(np.float32)).astype(np.float32)
    angle = np.tile(np.concatenate([angle, angle], 0), (P // hd, 1))
    sign = np.where((rows % hd) < hd // 2, -1.0, 1.0)[:, None]
    c["cos_sin"] = np.stack([np.cos(angle), np.sin(angle) * sign], 1).astype(np.float32)
    return c


def lay_out(i):
    f = {k: np.ascontiguousarray(v) for k, v in i.items()}
    d = {"x": f["x"], "mask_BxS2_if1": f["mask_BxS2_if1"]}
    ctx = f["ctx_2048"]
    d["ctxT"] = np.ascontiguousarray(ctx.transpose(2, 0, 1).reshape(KT, P, B, T).transpose(1, 0, 2, 3))
    wqkv, bqkv = f["L1_attn_Wqkv"], f["L1_attn_bqkv"]
    swap = (np.arange(D) // 16) * 16 + (np.arange(D) + 8) % 16
    for name, k in (("a1_wq", 0), ("a1_wk", 1)):
        m = wqkv[k * D:(k + 1) * D]
        d[name] = contraction_major(np.concatenate([m, m[swap]], 0).T)
    d["a1_wv"] = contraction_major(wqkv[2 * D:].T)
    d["a1_wo"] = contraction_major(f["L1_attn_Wo"].T)
    d["a1_bias"] = np.concatenate([bqkv[:D], bqkv[:D][swap], bqkv[D:2 * D], bqkv[D:2 * D][swap], bqkv[2 * D:],
                                   f["L1_attn_bo"]])[None]
    d["c1_wq"] = contraction_major(f["L1_xattn_w_q"].T)
    d["c1_wk"] = contraction_major(np.repeat(f["L1_xattn_w_k"].reshape(8, 1, 8, D), 4, axis=1).reshape(D, D).T)
    d["c1_wv"] = contraction_major(f["L1_xattn_w_v"].T)
    d["c1_wo"] = contraction_major(f["L1_xattn_w_o"].T)
    d["c1_bias"] = np.concatenate([np.zeros(3 * D, np.float32), f["L1_xattn_b_o"]])[None]
    H = 16
    per_head = [f[f"L0_attn_W{k}"].T.reshape(KT, P, H, P) for k in "qkvag"] + [f["L0_attn_Wb"].T.reshape(KT, P, H, 1)]
    cols = np.concatenate(per_head, -1).transpose(2, 1, 0, 3).reshape(H, P, KT * 641)
    taps = [f[f"L0_attn_conv_{k}_w"].reshape(H, P, 4) for k in "qkv"]
    rows = [f[f"L0_attn_conv_{k}_b"].reshape(H, P, 1) for k in "qkv"] + [f["L0_attn_ba"].reshape(H, P, 1)]
    bb = np.repeat(f["L0_attn_bb"].reshape(H, 1, 1), P, axis=1)
    d["a0_w"] = np.concatenate([cols, *taps, *rows, bb], -1)
    d["a0_wo"] = contraction_major(f["L0_attn_Wo"].T)
    d["a0_ln"] = np.stack([f["L0_attn_ln_g"], f["L0_attn_ln_b"]], 1)
    d["ctx_2048"] = ctx
    d["c0_wq"], d["c0_wk"], d["c0_wv"] = (np.ascontiguousarray(f[f"L0_xattn_W{k}"].T) for k in "qkv")
    d["c0_bias"] = np.concatenate([f["L0_xattn_bq"], f["L0_xattn_bk"], f["L0_xattn_bv"]])[None]
    d["c0_mask"] = f["mask_Bx1x2048_fk1"][:, 0]
    d["c0_mask_col"] = np.ascontiguousarray(f["mask_Bx1x2048_fk1"][:, 0].reshape(B, 2, P).transpose(2, 1, 0))
    hidden = 16 * 176 + 704
    fill = -hidden % P
    beside = lambda a: a.transpose(1, 0, 2).reshape(D, 16 * 176)
    pad_cols = np.zeros((D, fill), np.float32)
    d["e1_wg"] = contraction_major(np.concatenate([beside(f["L1_ffn_w_gate"]), f["L1_ffn_sh_gate"], pad_cols], 1))
    d["e1_wu"] = contraction_major(np.concatenate([beside(f["L1_ffn_w_up"]), f["L1_ffn_sh_up"], pad_cols], 1))
    d["e1_wd"] = contraction_major(np.concatenate([f["L1_ffn_w_down"].reshape(16 * 176, D), f["L1_ffn_sh_down"], pad_cols.T], 0))
    d["e1_wr"] = contraction_major(np.concatenate([f["L1_ffn_router_w"].T, f["L1_ffn_sh_gate_w"]], 1))
    expert = np.minimum(np.arange(hidden + fill) // 176, 16)
    d["e1_expert_rows"] = (expert[None, :] == np.arange(17)[:, None]).astype(np.float32)
    order = np.arange(2048).reshape(8, P, 2).transpose(0, 2, 1).ravel()
    down = f["L0_ffn_down_W_packed"].T.reshape(8, P, D).transpose(1, 0, 2).reshape(P, 2048)
    d["m0_codes"] = np.stack([f["L0_ffn_gate_W_packed"][order].T, f["L0_ffn_up_W_packed"][order].T, down], 1)
    down = f["L0_ffn_down_scales"].T.reshape(8, 8, D).transpose(1, 0, 2).reshape(8, 2048)
    d["m0_scales"] = np.stack([f["L0_ffn_gate_scales"][order].T, f["L0_ffn_up_scales"][order].T, down], 1)
    d.update(constants())
    return d


def kernel(**inputs):
    import concourse.bacc as bacc
    from concourse.bass_utils import run_bass_kernel_spmd as run

    nc = bacc.Bacc("TRN2", target_bir_lowering=False, num_devices=1)
    arrays = {f"in_{k}": np.ascontiguousarray(v) for k, v in lay_out(inputs).items()}
    dram = {k[3:]: nc.dram_tensor(k, v.shape, mybir.dt.from_np(v.dtype), kind="ExternalInput").ap()
            for k, v in arrays.items()}
    out = nc.dram_tensor("out", (B, T, D), F32, kind="ExternalOutput").ap()
    build(nc, dram, out)
    r = run(nc, [arrays], core_ids=[0])
    return r.results[0]["out"]
```

```python
from contextlib import ExitStack

import numpy as np

import concourse.bass as bass
from concourse import mybir

STAGES = (0, 1, 2, 3, 4, 5)

F32 = mybir.dt.float32
F32R = mybir.dt.float32r
I32 = mybir.dt.int32
ALU = mybir.AluOpType
ACT = mybir.ActivationFunctionType
AX = mybir.AxisListType.X

B, T, D = 16, 128, 256
P = 128
KT = D // P
BANK = 512
EPS = 1e-5
MASKED = -1.0e30


class Steps:

    def __init__(self, eng, sem, per_turn=0):
        self.eng, self.sem, self.per_turn, self.k, self.base = eng, sem, per_turn, 0, 0

    def turn(self, n):
        self.base, self.k = n * self.per_turn, 0

    def did(self, ins):
        ins.then_inc(self.sem, 1)
        self.k += 1
        return ins

    def wait(self):
        self.eng.wait_ge(self.sem, self.base + self.k)

    def end(self):
        assert self.k == self.per_turn, (self.k, self.per_turn)


class Section:

    def __init__(self, nc, stack, prefix):
        self.nc, self.stack, self.prefix, self.sems = nc, stack, prefix, []

    def sb(self, name, shape, dt=F32):
        return self.stack.enter_context(self.nc.sbuf_tensor(f"{self.prefix}_{name}", shape, dt))

    def sem(self, name):
        self.sems.append(self.stack.enter_context(self.nc.semaphore(f"{self.prefix}_{name}")))
        return self.sems[-1]

    def close(self):
        with self.nc.Block() as block:

            @block.gpsimd
            def _(pool):
                for sem in self.sems:
                    pool.sem_clear(sem)


def norm_stats(nc, g, prefix):
    with ExitStack() as st:
        s = Section(nc, st, prefix)
        stats = s.sb("stats", [P, B, 6])
        var_root = s.sb("var_root", [P, B])
        stats_done, aggregated = s.sem("stats_done"), s.sem("aggregated")
        rooted, inverted = s.sem("rooted"), s.sem("inverted")
        with nc.Block() as block:

            @block.vector
            def _(dve):
                with dve.Fori(0, B) as b:
                    dve.bn_stats(stats[:, bass.ds(b, 1), :], g.x[:, bass.ds(b, 1), :]).then_inc(stats_done, 1)
                dve.wait_ge(stats_done, B)
                for b in range(B):
                    dve.bn_aggr(g.mean_var[:, b, :], stats[:, b, :]).then_inc(aggregated, 1)
                dve.wait_ge(rooted, 1)
                dve.reciprocal(g.rstd[:, :], var_root[:, :]).then_inc(inverted, 1)
                dve.wait_ge(inverted, 1)

            @block.scalar
            def _(act):
                act.wait_ge(aggregated, B)
                act.activation(var_root[:, :], g.mean_var[:, :, 1], ACT.Sqrt, bias=g.eps[:, 0:1]).then_inc(rooted, 1)
        s.close()


def normalize(dve, g, out, n):
    return dve.tensor_scalar(out, g.x[:, bass.ds(n, 1), :], g.mean_var[:, bass.ds(n, 1), 0],
                             g.rstd[:, bass.ds(n, 1)], ALU.subtract, ALU.mult)


def bcast(ap, axis, count):
    shape = list(ap.shape)
    return ap.unsqueeze(axis).broadcast_to(shape[:axis] + [count] + shape[axis:])


def causal_attention(nc, g, prefix, heads, hd, rope, kv_from_ctx, w):
    per_block = 32 // hd
    per_tile = P // hd
    unit_heads = 4
    units = heads // unit_heads
    halves = 2 if rope else 1
    kv_heads = heads if not kv_from_ctx else heads // per_block
    scale = float(hd) ** -0.5
    dve_steps_a_turn = 1 + (2 if rope else 0) + units + 2 * 1 + 1
    if per_block == 2:
        unit_blocks = [[(0, j), (1, j)] for j in range(4)]
    else:
        unit_blocks = [[(t, j)] for t in range(KT) for j in range(4)]

    with ExitStack() as st:
        s = Section(nc, st, prefix)
        wq = s.sb("wq", [P, KT, halves * D])
        wk = s.sb("wk", [P, KT, halves * D])
        wv = s.sb("wv", [P, KT, kv_heads * hd])
        wo = s.sb("wo", [P, KT, D])
        bias_rows = s.sb("bias_rows", [1, 2 * halves * D + 2 * D])
        cos_sin = s.sb("cos_sin", [P, 2, T])
        head_rows = s.sb("head_rows", [P, per_block])
        causal = s.sb("causal", [P, T])
        mask = s.sb("mask", [P, T])
        pad_int = s.sb("pad_int", [P, B, T], I32)
        pad = s.sb("pad", [P, B, T])
        xn = s.sb("xn", [P, D])
        xnT = s.sb("xnT", [P, KT, T])
        ctxT = s.sb("ctxT", [P, KT, T])
        rope_a = s.sb("rope_a", [P, 2, KT, T])
        rope_b = s.sb("rope_b", [P, 2, KT, T])
        qT = s.sb("qT", [P, KT, T])
        kT = s.sb("kT", [P, KT, T])
        k_spread = s.sb("k_spread", [P, KT, per_block, T])
        v_one = s.sb("v_one", [P, kv_heads, hd + 1])
        probs = s.sb("probs", [P, 2, unit_heads, T])
        peak = s.sb("peak", [P, 2, unit_heads])
        probsT = s.sb("probsT", [P, 2, unit_heads, T])
        recip = s.sb("recip", [P, heads])
        y = s.sb("y", [P, D])
        yT = s.sb("yT", [P, KT, T])

        loaded, ctx_loaded = s.sem("loaded"), s.sem("ctx_loaded")
        ones_set, pad_made, mask_made = s.sem("ones_set"), s.sem("pad_made"), s.sem("mask_made")
        normed, xnT_psum, xnT_done = s.sem("normed"), s.sem("xnT_psum"), s.sem("xnT_done")
        projected, v_done = s.sem("projected"), s.sem("v_done")
        roped, q_done, k_summed, k_done = s.sem("roped"), s.sem("q_done"), s.sem("k_summed"), s.sem("k_done")
        scored, scaled, peaked, shifted = s.sem("scored"), s.sem("scaled"), s.sem("peaked"), s.sem("shifted")
        expd, turned, turned_out = s.sem("expd"), s.sem("turned"), s.sem("turned_out")
        weighed, inverted, y_done = s.sem("weighed"), s.sem("inverted"), s.sem("y_done")
        y_turned, yT_done, out_psum, added = s.sem("y_turned"), s.sem("yT_done"), s.sem("out_psum"), s.sem("added")

        px, pq, pk = g.banks[0], g.banks[1], g.banks[2]
        p_scores = [g.banks[3], g.banks[4]]
        p_turned = [g.banks[5], g.banks[6]]
        p_av = g.banks[7]
        av = p_av[:, 0:heads * (hd + 1)].rearrange("p (h e) -> p h e", e=hd + 1)
        n_loads = 7 + (3 if rope else 0) + (1 if kv_from_ctx else 0) - (0 if rope else 0)

        with nc.Block() as block:

            @block.sync
            def _(sp):
                loads = [(wq, w["wq"]), (wk, w["wk"]), (wv, w["wv"]), (wo, w["wo"]),
                         (head_rows, w["head_rows"]), (causal, w["causal"]), (bias_rows, w["bias_rows"])]
                for dst, src in loads:
                    sp.dma_start(dst[:], src).then_inc(loaded, 16)
                if rope:
                    sp.dma_start(cos_sin[:], w["cos_sin"]).then_inc(loaded, 16)
                if kv_from_ctx:
                    sp.dma_start(pad_int[:], w["pad"].partition_broadcast(P)).then_inc(loaded, 16)
                    with sp.Fori(0, B) as n:
                        sp.wait_ge(added, n + 1)
                        sp.dma_start(ctxT[:, :, :], w["ctxT"][:, :, bass.ds(n, 1), :]).then_inc(ctx_loaded, 16)
                    sp.wait_ge(ctx_loaded, 16 * B)

            all_loads = 16 * 8

            @block.vector
            def _(dve):
                dve.sem_inc(added, 1)
                dve.memset(v_one[:, :, hd:hd + 1], 1.0).then_inc(ones_set, 1)
                dve.wait_ge(loaded, all_loads)
                if kv_from_ctx:
                    dve.tensor_scalar(pad[:, :, :], pad_int[:, :, :], 0, MASKED, ALU.is_equal, ALU.mult)\
                       .then_inc(pad_made, 1)
                with dve.Fori(0, B) as n:
                    dve.wait_ge(added, n + 1)
                    normalize(dve, g, xn[:, :], n).then_inc(normed, 1)
                    dve.wait_ge(projected, 2 * n + 1)
                    if rope:
                        for c, bank in enumerate((pq, pk)):
                            src = bank[:, :].rearrange("p (f c t) -> p f c t", f=2, c=KT)
                            dve.tensor_tensor(rope_a[:, c], src[:, 0], bcast(cos_sin[:, 0, :], 1, KT), ALU.mult)
                            dve.tensor_tensor(rope_b[:, c], src[:, 1], bcast(cos_sin[:, 1, :], 1, KT), ALU.mult)\
                               .then_inc(roped, 1)
                        dve.wait_ge(k_summed, n + 1)
                        k_rows = kT[:, :, :]
                    else:
                        k_rows = pk[:, 0:D].rearrange("p (c t) -> p c t", c=KT)
                    for c in range(KT):
                        ins = dve.tensor_tensor(k_spread[:, c], bcast(k_rows[:, c, :], 1, per_block),
                                                bcast(head_rows[:, :], 2, T), ALU.mult)
                    ins.then_inc(k_done, 1)
                    for u in range(units):
                        dve.wait_ge(scored, n * units + u + 1)
                        if u == 0 and kv_from_ctx:
                            dve.wait_ge(mask_made, n + 1)
                        if u >= 2:
                            dve.wait_ge(turned, n * units + u - 1)
                        m = mask if kv_from_ctx else causal
                        dve.scalar_tensor_tensor(probs[:, u % 2], p_scores[u % 2][:, :].rearrange("p (h t) -> p h t", t=T),
                                                 scale, bcast(m[:, :], 1, unit_heads), ALU.mult, ALU.add)\
                           .then_inc(scaled, 1)
                        dve.wait_ge(scaled, n * units + u + 1)
                        dve.tensor_reduce(peak[:, u % 2], probs[:, u % 2], AX, ALU.max).then_inc(peaked, 1)
                    dve.wait_ge(weighed, n * units + units)
                    dve.reciprocal(recip[:, :], av[:, :, hd]).then_inc(inverted, 1)
                    dve.wait_ge(inverted, n + 1)
                    dve.tensor_tensor(y[:, :].rearrange("p (h e) -> p h e", e=hd), av[:, :, 0:hd],
                                      bcast(recip[:, :], 2, hd), ALU.mult).then_inc(y_done, 1)
                    dve.wait_ge(out_psum, n + 1)
                    dve.tensor_tensor(g.x[:, bass.ds(n, 1), :], g.x[:, bass.ds(n, 1), :], pq[:, 0:D], ALU.add)\
                       .then_inc(added, 1)

            @block.gpsimd
            def _(pool):
                if kv_from_ctx:
                    pool.wait_ge(loaded, all_loads)
                    pool.wait_ge(pad_made, 1)
                with pool.Fori(0, B) as n:
                    if kv_from_ctx:
                        pool.wait_ge(normed, n + 1)
                        pool.tensor_tensor(mask[:, :], causal[:, :], pad[:, bass.ds(n, 1), :], ALU.add)\
                            .then_inc(mask_made, 1)
                    if rope:
                        pool.wait_ge(roped, 2 * n + 1)
                        pool.tensor_tensor(qT[:, :, :], rope_a[:, 0], rope_b[:, 0], ALU.add).then_inc(q_done, 1)
                        pool.wait_ge(roped, 2 * n + 2)
                        pool.tensor_tensor(kT[:, :, :], rope_a[:, 1], rope_b[:, 1], ALU.add).then_inc(k_summed, 1)
                    for u in range(units):
                        pool.wait_ge(peaked, n * units + u + 1)
                        pool.tensor_tensor(probs[:, u % 2], probs[:, u % 2], bcast(peak[:, u % 2], 2, T),
                                           ALU.subtract).then_inc(shifted, 1)

            @block.scalar
            def _(act):
                with act.Fori(0, B) as n:
                    act.wait_ge(xnT_psum, n + 1)
                    act.copy(xnT[:, :, :], px[:, 0:D].rearrange("p (c t) -> p c t", c=KT)).then_inc(xnT_done, 1)
                    act.wait_ge(projected, 2 * n + 2)
                    if not rope:
                        act.copy(qT[:, :, :], pq[:, 0:D].rearrange("p (c t) -> p c t", c=KT)).then_inc(q_done, 1)
                    act.wait_ge(ones_set, 1)
                    act.copy(v_one[:, :, 0:hd], px[:, D:D + kv_heads * hd].rearrange("p (h e) -> p h e", e=hd))\
                       .then_inc(v_done, 1)

                    def turn_out(u):
                        act.wait_ge(turned, n * units + u + 1)
                        if u >= 2:
                            act.wait_ge(weighed, n * units + u - 1)
                        act.copy(probsT[:, u % 2], p_turned[u % 2][:, :].rearrange("p (h t) -> p h t", t=T))\
                           .then_inc(turned_out, 1)

                    for u in range(units):
                        act.wait_ge(shifted, n * units + u + 1)
                        act.activation(probs[:, u % 2], probs[:, u % 2], ACT.Exp).then_inc(expd, 1)
                        if u >= 1:
                            turn_out(u - 1)
                    turn_out(units - 1)
                    act.wait_ge(y_turned, n + 1)
                    act.copy(yT[:, :, :], px[:, 0:D].rearrange("p (c t) -> p c t", c=KT)).then_inc(yT_done, 1)

            @block.tensor
            def _(pe):
                pe.wait_ge(loaded, all_loads)
                q_bias, k_bias = 0, halves * D
                v_bias, o_bias = 2 * halves * D, 2 * halves * D + D
                with pe.Fori(0, B) as n:
                    pe.wait_ge(normed, n + 1)
                    for c in range(KT):
                        ins = pe.transpose(px[:, c * T:(c + 1) * T], xn[:, c * P:(c + 1) * P], g.ident[:, :])
                    ins.then_inc(xnT_psum, 1)
                    pe.wait_ge(xnT_done, n + 1)
                    if kv_from_ctx:
                        pe.wait_ge(ctx_loaded, 16 * n + 16)
                    kv_src = ctxT if kv_from_ctx else xnT
                    for bank, wt, off, src in ((pq, wq, q_bias, xnT), (pk, wk, k_bias, kv_src)):
                        for f in range(halves * KT):
                            o = bank[:, f * T:(f + 1) * T]
                            for c in range(KT):
                                ins = pe.matmul(o, wt[:, c, f * P:(f + 1) * P], src[:, c, :],
                                                start=(c == 0), stop=(c == KT - 1 and not rope))
                            if rope:
                                ins = pe.matmul(o, bias_rows[0:1, off + f * P:off + (f + 1) * P], g.ones[0:1, 0:T],
                                                start=False, stop=True)
                    ins.then_inc(projected, 1)
                    o = px[:, D:D + kv_heads * hd]
                    for c in range(KT):
                        ins = pe.matmul(o, kv_src[:, c, :], wv[:, c, :], start=(c == 0), stop=(c == KT - 1 and not rope))
                    if rope:
                        ins = pe.matmul(o, g.ones[0:1, 0:T], bias_rows[0:1, v_bias:v_bias + D], start=False, stop=True)
                    ins.then_inc(projected, 1)

                    def scores(u):
                        if u == 0:
                            pe.wait_ge(q_done, n + 1)
                            pe.wait_ge(k_done, n + 1)
                        if u >= 2:
                            pe.wait_ge(peaked, n * units + u - 1)
                        width = BANK // len(unit_blocks[u])
                        for i, (c, j) in enumerate(unit_blocks[u]):
                            rows = slice(32 * j, 32 * j + 32)
                            ins = pe.matmul(p_scores[u % 2][:, i * width:(i + 1) * width], qT[rows, c, :],
                                            k_spread[rows, c, :, :], start=True, stop=True)
                        ins.then_inc(scored, 1)

                    def turn(u):
                        pe.wait_ge(expd, n * units + u + 1)
                        if u >= 2:
                            pe.wait_ge(turned_out, n * units + u - 1)
                        for h in range(unit_heads):
                            ins = pe.transpose(p_turned[u % 2][:, h * T:(h + 1) * T], probs[:, u % 2, h, :], g.ident[:, :])
                        ins.then_inc(turned, 1)

                    def weigh(u):
                        if u == 0:
                            pe.wait_ge(v_done, n + 1)
                        pe.wait_ge(turned_out, n * units + u + 1)
                        unit = [c * per_tile + j * per_block + k for c, j in unit_blocks[u] for k in range(per_block)]
                        for i, h in enumerate(unit):
                            kv = h // per_block if kv_from_ctx else h
                            ins = pe.matmul(av[:, h, :], probsT[:, u % 2, i, :], v_one[:, kv, :], start=True, stop=True)
                        ins.then_inc(weighed, 1)

                    scores(0)
                    scores(1)
                    turn(0)
                    for u in range(1, units):
                        if u + 1 < units:
                            scores(u + 1)
                        turn(u)
                        weigh(u - 1)
                    weigh(units - 1)
                    pe.wait_ge(y_done, n + 1)
                    for c in range(KT):
                        ins = pe.transpose(px[:, c * T:(c + 1) * T], y[:, c * P:(c + 1) * P], g.ident[:, :])
                    ins.then_inc(y_turned, 1)
                    pe.wait_ge(yT_done, n + 1)
                    for c in range(KT):
                        pe.matmul(pq[:, 0:D], yT[:, c, :], wo[:, c, :], start=(c == 0), stop=False)
                    pe.matmul(pq[:, 0:D], g.ones[0:1, 0:T], bias_rows[0:1, o_bias:o_bias + D],
                              start=False, stop=True).then_inc(out_psum, 1)
        s.close()


def layer1_attention(nc, g):
    norm_stats(nc, g, "n3")
    w = dict(wq=g.dram["a1_wq"], wk=g.dram["a1_wk"], wv=g.dram["a1_wv"], wo=g.dram["a1_wo"],
             head_rows=g.dram["head_rows16"], causal=g.dram["causal"], bias_rows=g.dram["a1_bias"],
             cos_sin=g.dram["cos_sin"])
    causal_attention(nc, g, "a1", 16, 16, True, False, w)


def layer1_cross(nc, g):
    norm_stats(nc, g, "n4")
    w = dict(wq=g.dram["c1_wq"], wk=g.dram["c1_wk"], wv=g.dram["c1_wv"], wo=g.dram["c1_wo"],
             head_rows=g.dram["head_rows8"], causal=g.dram["causal"], bias_rows=g.dram["c1_bias"],
             pad=g.dram["mask_BxS2_if1"], ctxT=g.dram["ctxT"])
    causal_attention(nc, g, "c1", 32, 8, False, True, w)



class Count:

    def __init__(self, sem, per_turn, start=0, by=1):
        self.sem, self.per_turn, self.start, self.by = sem, per_turn, start, by

    def wait(self, eng, n, k):
        assert k + self.start > 0
        eng.wait_ge(self.sem, n * (self.per_turn * self.by) + (k + self.start) * self.by)

    def rise(self, ins):
        return ins.then_inc(self.sem, self.by)

    def open(self, eng):
        eng.sem_inc(self.sem, self.start * self.by)


def layer0_attention(nc, g):
    norm_stats(nc, g, "n0")
    H, HD = 16, P
    TURNS = B // 2
    N2 = 2 * T
    CH = 16
    NC = T // CH
    PERIOD, LAG = 27, 13
    LAST_PART = PERIOD - CH - 2
    LEVELS = CH.bit_length() - 1
    W_COLS, N_SCALARS = KT * 641, 17
    KIND_K, KIND_Q = range(2)
    ROWS = 32
    k_scale = float(HD) ** -0.5

    with ExitStack() as st:
        s = Section(nc, st, "a0")
        wbuf = [s.sb(f"wbuf{p}", [P, W_COLS]) for p in range(2)]
        scalars = s.sb("scalars", [P, H, N_SCALARS])
        xn = s.sb("xn", [P, 2, D])
        xnT = s.sb("xnT", [P, KT, N2])
        raw = [s.sb(f"raw{p}", [P, 3, 2, T + 3]) for p in range(2)]
        acc = [s.sb(f"acc{p}", [P, 3, 2, T]) for p in range(2)]
        beta = [s.sb(f"beta{p}", [P, 2, T]) for p in range(2)]
        q_h = [s.sb(f"q{p}", [P, 2, T]) for p in range(2)]
        k_h = [s.sb(f"k{p}", [P, 2, T]) for p in range(2)]
        kb_h = [s.sb(f"kb{p}", [P, 2, T + 1]) for p in range(2)]
        vb = s.sb("vb", [P, 2, H, T])
        decay = s.sb("decay", [P, 2, H, T])
        gate = s.sb("gate", [P, 2, H, T])
        dots = s.sb("dots", [P, 2, H, 2, T])
        near = s.sb("near", [P, 2, 2, 2, ROWS, H])
        near_r = s.sb("near_r", [P, 2, 2, 2, ROWS, H], F32R)
        pair = s.sb("pair", [P, 2, ROWS], F32R)
        second = s.sb("second", [P, 1])
        past = s.sb("past", [P, 2, H, T])
        live = s.sb("live", [P, 2, 2, CH, H])
        since = s.sb("since", [P, 2, 2, H, CH + 1])
        pastT = s.sb("pastT", [P, 2, 4, P])
        y0 = s.sb("y0", [P, 2, H, 2 * CH])
        prod = s.sb("prod", [P, 2, 2, H * CH])
        sums = s.sb("sums", [P, 2, 2, CH + 1, H])
        yq = s.sb("yq", [P, 2, H, CH])
        ln = s.sb("ln", [P, 2])
        wo = dots[:, 0, :, :, :].rearrange("p a b c -> p (a b c)").rearrange("p (h d) -> p h d", h=H)
        square = [past[:, 0, 0:4, :], past[:, 0, 4:8, :]]
        root = [past[:, 0, 8:12, :], past[:, 0, 12:16, :]]

        def sig_of(p):
            return raw[p][:, :, :, 3:]

        def counts(name, per_turn, start=0, by=1):
            return Count(s.sem(name), per_turn, start, by)

        w_loaded = [counts(f"w_loaded{p}", H // 2, by=16) for p in range(2)]
        ln_loaded, wo_loaded = s.sem("ln_loaded"), counts("wo_loaded", 1, by=16)
        set_up = s.sem("set_up")
        normed, xnT_psum, xnT_done = counts("normed", 2), counts("xnT_psum", 1), counts("xnT_done", 1)
        projected, raw_done, gates_done = counts("projected", H, 2), counts("raw_done", H), counts("gates_done", H, 2)
        conv_step, sig_done = counts("conv_step", 4 * H), counts("sig_done", H, 2)
        k_done, qkv_done = counts("k_done", H), counts("qkv_done", H, 2)
        pool_step = counts("pool_step", H)
        dotted, dots_out = [counts(f"dotted{b}", H) for b in range(2)], [counts(f"dots_out{b}", H, 1) for b in range(2)]
        high_part, split = [counts(f"high_part{b}", 1) for b in range(2)], [counts(f"split{b}", 1) for b in range(2)]
        spread = [counts(f"spread{b}", NC * CH) for b in range(2)]
        multiplied = [counts(f"multiplied{b}", NC * CH) for b in range(2)]
        summed = [counts(f"summed{b}", NC * CH) for b in range(2)]
        u_done = [counts(f"u_done{b}", NC * CH) for b in range(2)]
        decayed = [counts(f"decayed{b}", NC * (CH - 1)) for b in range(2)]
        since_copied = [counts(f"since_copied{b}", NC - 1) for b in range(2)]
        since_done = [counts(f"since_done{b}", (NC - 1) * LEVELS) for b in range(2)]
        yk_done = [counts(f"yk_done{b}", 2 * (NC - 1)) for b in range(2)]
        yq_done = [counts(f"yq_done{b}", NC - 1) for b in range(2)]
        o_done = [counts(f"o_done{b}", NC) for b in range(2)]
        yq_zero = counts("yq_zero", 1)
        joined = [counts(f"joined{b}", NC - 1) for b in range(2)]
        past_decayed = [counts(f"past_decayed{b}", 4 * (NC - 2)) for b in range(2)]
        past_turned, past_out = counts("past_turned", 8 * (NC - 1)), counts("past_out", 8 * (NC - 1))
        past_used = counts("past_used", 8 * (NC - 1))
        y0_out = [counts(f"y0_out{b}", NC - 1) for b in range(2)]
        mean_psum, centred, squared = counts("mean_psum", 8), counts("centred", 8), counts("squared", 8)
        var_psum, rooted, inverted = counts("var_psum", 8), counts("rooted", 8), counts("inverted", 8)
        normal, gated = counts("normal", 8), counts("gated", 8)
        out_psum, added = counts("out_psum", 2), counts("added", 2, 2)

        p_proj = [[g.banks[3 * p + i] for i in range(3)] for p in range(2)]
        p_dots = [g.banks[6], g.banks[7]]
        p_spread = [[g.banks[0], g.banks[1]], [g.banks[2], g.banks[3]]]
        p_past, p_y0 = [g.banks[4], g.banks[5]], [g.banks[6], g.banks[7]]
        p_mean, p_var, p_out = [g.banks[0], g.banks[1]], [g.banks[2], g.banks[3]], [g.banks[4], g.banks[5]]

        def slots():
            for slot in range(PERIOD * NC + LAG):
                steps, parts = [], []
                for b in range(2):
                    m, r = divmod(slot - LAG * b, PERIOD)
                    if 0 <= m < NC and r <= CH:
                        steps.append((b, m, r))
                    elif 0 <= m < NC - 1:
                        parts.append((b, m, r - CH - 1))
                yield slot, steps, parts

        def pieces(part):
            order = [("turn", 0), ("turn", 1), ("product", 0), ("turn", 2), ("product", 1), ("turn", 3), ("product", 2), ("product", 3)]
            work, done = {"turn": 1, "product": 2}, 0
            total = 4 * sum(work[kind] for kind, _ in order)
            for kind, group in order:
                for i in range(4):
                    if done * LAST_PART // total == part:
                        yield kind, group, i
                    done += work[kind]

        def scalar(h, k):
            return scalars[:, h, k:k + 1]

        with nc.Block() as block:

            @block.sync
            def _(sp):
                sp.dma_start(ln[:, :], g.dram["a0_ln"]).then_inc(ln_loaded, 16)
                sp.dma_start(scalars[:, :, :], g.dram["a0_w"][:, :, W_COLS:].rearrange("h p c -> p h c")).then_inc(ln_loaded, 16)
                with sp.Fori(0, TURNS) as n:
                    for h in range(H):
                        projected.wait(sp, n, h - 1)
                        w_loaded[h % 2].rise(sp.dma_start(wbuf[h % 2][:, :], g.dram["a0_w"][h, :, 0:W_COLS]))
                    for b in range(2):
                        spread[b].wait(sp, n, NC * CH)
                    wo_loaded.rise(sp.dma_start(wo, g.dram["a0_wo"]))
                for p in range(2):
                    sp.wait_ge(w_loaded[p].sem, 16 * TURNS * H // 2)
                sp.wait_ge(wo_loaded.sem, 16 * TURNS)

            @block.vector
            def _(dve):
                added.open(dve)
                for p in range(2):
                    dve.memset(raw[p][:, :, :, 0:3], 0.0).then_inc(set_up, 1)
                dve.memset(past[:, :, :, :], 0.0).then_inc(set_up, 1)
                dve.memset(since[:, :, :, :, 0:1], 1.0).then_inc(set_up, 1)
                for p in range(2):
                    dve.memset(kb_h[p][:, :, T:T + 1], 0.0).then_inc(set_up, 1)
                blocks = g.ident[:, :].rearrange("p (a c i) -> p a c i", a=2, c=2)
                dve.tensor_tensor(pair[:, :, :], blocks[:, :, 0], blocks[:, :, 1], ALU.add).then_inc(set_up, 1)
                dve.memset(second[:, :], 0.0).then_inc(set_up, 1)
                dve.wait_ge(set_up, 8)
                for p0 in (ROWS, 3 * ROWS):
                    dve.memset(second[p0:p0 + ROWS, :], -1.0).then_inc(set_up, 1)
                dve.wait_ge(set_up, 10)
                dve.wait_ge(ln_loaded, 32)

                def convolve(n, h):
                    p = h % 2
                    raw_done.wait(dve, n, h + 1)
                    qkv_done.wait(dve, n, h - 1)
                    for c in range(3):
                        ins = dve.tensor_scalar(acc[p][:, c], raw[p][:, c, :, 3:], scalar(h, 4 * c + 3), scalar(h, 12 + c),
                                                ALU.mult, ALU.add)
                    conv_step.rise(ins)
                    if h >= 1:
                        make_k(n, h - 1)
                    for j in (2, 1, 0):
                        conv_step.wait(dve, n, 4 * h + 3 - j)
                        for c in range(3):
                            ins = dve.scalar_tensor_tensor(acc[p][:, c], raw[p][:, c, :, j:j + T], scalar(h, 4 * c + j),
                                                           acc[p][:, c], ALU.mult, ALU.add)
                        conv_step.rise(ins)

                def make_k(n, h):
                    p = h % 2
                    sig_done.wait(dve, n, h + 1)
                    if h >= 2:
                        dots_out[1].wait(dve, n, h - 1)
                    k_done.rise(dve.scalar_tensor_tensor(k_h[p][:, :, :], acc[p][:, 1], k_scale, sig_of(p)[:, 1], ALU.mult, ALU.mult))

                def step(n, b, m, j):
                    e = m * CH + j
                    first = 0 if j < CH else 1

                    def multiply():
                        if j == 0:
                            return
                        spread[b].wait(dve, n, e)
                        if j > 1:
                            decayed[b].wait(dve, n, m * (CH - 1) + j - 1)
                        u_done[b].wait(dve, n, e)
                        view = prod[:, b, :, 0:H * j].rearrange("p c (i h) -> p c i h", i=j)
                        rows = p_spread[b][j % 2][:, 0:2 * H * j].rearrange("p (c i h) -> p c i h", c=2, i=j)
                        us = bcast(live[:, b, j % 2, 0:j, :], 1, 2)
                        multiplied[b].rise(dve.tensor_tensor(view[:, first:], us[:, first:], rows[:, first:], ALU.mult))

                    def total():
                        if j == 0:
                            return
                        multiplied[b].wait(dve, n, e)
                        if j == 1 and m > 0:
                            o_done[b].wait(dve, n, m)
                        view = prod[:, b, :, 0:H * j].rearrange("p c (i h) -> p c h i", i=j)
                        summed[b].rise(dve.tensor_reduce(sums[:, b, first:, j, :], view[:, first:], AX, ALU.add))

                    def update():
                        if j == CH:
                            return
                        new = live[:, b, (j + 1) % 2, j, :]
                        if j == 0:
                            if m > 0:
                                chunk = vb[:, b, :, m * CH:(m + 1) * CH]
                                y0_out[b].wait(dve, n, m)
                                since_done[b].wait(dve, n, m * LEVELS)
                                yk = y0[:, b, :, 0:CH]
                                yk_done[b].rise(dve.tensor_tensor(yk, yk, since[:, b, m % 2, :, 0:CH], ALU.mult))
                                yk_done[b].wait(dve, n, 2 * m - 1)
                                yk_done[b].rise(dve.tensor_tensor(chunk, chunk, yk, ALU.subtract))
                                yk_done[b].wait(dve, n, 2 * m)
                            elif b == 0:
                                qkv_done.wait(dve, n, H)
                            ins = dve.tensor_copy(new, vb[:, b, :, e])
                        else:
                            summed[b].wait(dve, n, e)
                            ins = dve.tensor_tensor(new, vb[:, b, :, e], sums[:, b, 0, j, :], ALU.subtract)
                        u_done[b].rise(ins)

                    return multiply, total, update

                with dve.Fori(0, TURNS) as n:
                    added.wait(dve, n, 0)
                    for b in range(2):
                        normed.rise(normalize(dve, g, xn[:, b, :], 2 * n + b))
                    yq_zero.rise(dve.memset(yq[:, :, :, :], 0.0))
                    for h in range(H):
                        convolve(n, h)
                    make_k(n, H - 1)
                    high_part[0].wait(dve, n, 1)
                    split[0].rise(dve.scalar_tensor_tensor(near_r[:, 0], near_r[:, 0].bitcast(F32), second[:, 0:1], near[:, 0], ALU.mult, ALU.add))
                    high_part[1].wait(dve, n, 1)
                    split[1].rise(dve.scalar_tensor_tensor(near_r[:, 1], near_r[:, 1].bitcast(F32), second[:, 0:1], near[:, 1], ALU.mult, ALU.add))
                    for _, steps, _ in slots():
                        parts = [step(n, *x) for x in steps]
                        for i in range(3):
                            for x in parts:
                                x[i]()
                    def group(i):
                        b, q = divmod(i, 4)
                        return slice(4 * q, 4 * q + 4), b

                    def centre(i):
                        hs, b = group(i)
                        mean_psum.wait(dve, n, i + 1)
                        centred.rise(dve.scalar_tensor_tensor(vb[:, b, hs, :], p_mean[i % 2][:, :].rearrange("p (h t) -> p h t", t=T),
                                                              -1.0 / HD, vb[:, b, hs, :], ALU.mult, ALU.add))

                    def finish(i):
                        hs, b = group(i)
                        o = vb[:, b, hs, :]
                        rooted.wait(dve, n, i + 1)
                        inverted.rise(dve.reciprocal(root[i % 2], root[i % 2]))
                        inverted.wait(dve, n, i + 1)
                        normal.rise(dve.scalar_tensor_tensor(o, o, ln[:, 0:1], root[i % 2], ALU.mult, ALU.mult))
                        normal.wait(dve, n, i + 1)
                        gated.rise(dve.scalar_tensor_tensor(o, o, ln[:, 1:2], gate[:, b, hs, :], ALU.add, ALU.mult))

                    centre(0)
                    centre(1)
                    for i in range(8):
                        if i + 2 < 8:
                            centre(i + 2)
                        finish(i)
                    for b in range(2):
                        out_psum.wait(dve, n, b + 1)
                        added.rise(dve.tensor_tensor(g.x[:, bass.ds(2 * n + b, 1), :], g.x[:, bass.ds(2 * n + b, 1), :],
                                                     p_out[b][:, 0:D], ALU.add))

            @block.gpsimd
            def _(pool):
                qkv_done.open(pool)
                pool.wait_ge(set_up, 10)
                with pool.Fori(0, TURNS) as n:
                    normed.wait(pool, n, 2)
                    for h in range(H):
                        p = h % 2
                        sig_done.wait(pool, n, h + 1)
                        if h >= 2:
                            dots_out[1].wait(pool, n, h - 1)
                        pool.tensor_tensor(q_h[p][:, :, :], acc[p][:, 0], sig_of(p)[:, 0], ALU.mult)
                        pool_step.rise(pool.tensor_tensor(acc[p][:, 2], acc[p][:, 2], sig_of(p)[:, 2], ALU.mult))
                        pool_step.wait(pool, n, h + 1)
                        pool.tensor_tensor(vb[:, :, h, :], acc[p][:, 2], beta[p][:, :, :], ALU.mult)
                        k_done.wait(pool, n, h + 1)
                        qkv_done.rise(pool.tensor_tensor(kb_h[p][:, :, 0:T], k_h[p][:, :, :], beta[p][:, :, :], ALU.mult))

                    def step(b, m, j):
                        e = m * CH + j
                        if 1 <= j < CH:
                            k = m * (CH - 1) + j
                            u_done[b].wait(pool, n, e)
                            if j > 1:
                                decayed[b].wait(pool, n, k - 1)
                            decayed[b].rise(pool.tensor_tensor(live[:, b, (j + 1) % 2, 0:j, :], live[:, b, j % 2, 0:j, :],
                                                               bcast(decay[:, b, :, e], 1, j), ALU.mult))

                    def beside(b, m, j):
                        if m < NC - 1 and 2 <= j < 2 + LEVELS:
                            level = j - 2
                            size = 2 << level
                            if level == 0:
                                since_copied[b].wait(pool, n, m + 1)
                            else:
                                since_done[b].wait(pool, n, m * LEVELS + level)
                            groups = since[:, b, (m + 1) % 2, :, 1:CH + 1].rearrange("p h (g s) -> p h g s", s=size)
                            half = groups[:, :, :, size // 2:size]
                            since_done[b].rise(pool.tensor_tensor(half, half, groups[:, :, :, size // 2 - 1:size // 2].broadcast_to(
                                list(half.shape)), ALU.mult))
                        if 0 < m < NC - 1 and 7 <= j < 11:
                            part = j - 7
                            t0, hs = m * CH, slice(4 * part, 4 * part + 4)
                            past_turned.wait(pool, n, (2 * (m - 1) + b) * 4 + part + 1)
                            since_done[b].wait(pool, n, m * LEVELS)
                            past_decayed[b].rise(pool.tensor_tensor(past[:, b, hs, 0:t0], past[:, b, hs, 0:t0],
                                                                    bcast(since[:, b, m % 2, hs, CH], 2, t0), ALU.mult))
                        if j == CH:
                            e = (m + 1) * CH
                            summed[b].wait(pool, n, e)
                            if m > 0:
                                yq_done[b].wait(pool, n, m)
                            else:
                                yq_zero.wait(pool, n, 1)
                            o_done[b].rise(pool.tensor_tensor(
                                vb[:, b, :, m * CH:(m + 1) * CH], sums[:, b, 1, 1:CH + 1, :].rearrange("p t h -> p h t"),
                                yq[:, b, :, :], ALU.add))

                    def boundary(b, m, part):
                        if part == LAST_PART:
                            y0_out[b].wait(pool, n, m + 1)
                            o_done[b].wait(pool, n, m + 1)
                            since_done[b].wait(pool, n, (m + 1) * LEVELS)
                            yq_done[b].rise(pool.tensor_tensor(yq[:, b], y0[:, b, :, CH:2 * CH],
                                                               since[:, b, (m + 1) % 2, :, 1:CH + 1], ALU.mult))

                    for _, steps, parts in slots():
                        for x in steps:
                            step(*x)
                        for x in steps:
                            beside(*x)
                        for x in parts:
                            boundary(*x)

            @block.scalar
            def _(act):
                act.wait_ge(ln_loaded, 32)
                gates_done.open(act)
                sig_done.open(act)
                for b in range(2):
                    dots_out[b].open(act)
                act.wait_ge(set_up, 10)
                with act.Fori(0, TURNS) as n:

                    def evacuate(h):
                        p = h % 2
                        projected.wait(act, n, h + 1)
                        if h >= 2:
                            qkv_done.wait(act, n, h - 1)
                        act.copy(raw[p][:, 0:2, :, 3:], p_proj[p][0][:, :].rearrange("p (c b t) -> p c b t", c=2, b=2))
                        raw_done.rise(act.copy(raw[p][:, 2, :, 3:], p_proj[p][1][:, 0:N2].rearrange("p (b t) -> p b t", b=2)))
                        act.activation(decay[:, :, h, :], p_proj[p][1][:, N2:2 * N2].rearrange("p (b t) -> p b t", b=2),
                                       ACT.Sigmoid, bias=scalar(h, 15))
                        act.activation(gate[:, :, h, :], p_proj[p][2][:, 0:N2].rearrange("p (b t) -> p b t", b=2), ACT.Sigmoid)
                        gates_done.rise(act.activation(beta[p][:, :, :], p_proj[p][2][:, N2:2 * N2].rearrange("p (b t) -> p b t", b=2),
                                                       ACT.Sigmoid, bias=scalar(h, 16)))

                    def copy_dots(h):
                        for b in range(2):
                            dotted[b].wait(act, n, h + 1)
                            act.copy(near[:, b, :, :, :, h], p_dots[b][:, 0:4 * ROWS].rearrange("p (c a i) -> p c a i", c=2, a=2))
                            dots_out[b].rise(act.copy(dots[:, b, h, :, :], p_dots[b][:, BANK // 2:].rearrange("p (c t) -> p c t", c=2)))

                    xnT_psum.wait(act, n, 1)
                    xnT_done.rise(act.copy(xnT[:, :, :], g.banks[6][:, :].rearrange("p (c t) -> p c t", c=KT)))
                    evacuate(0)
                    for h in range(H):
                        if h + 1 < H:
                            evacuate(h + 1)
                        conv_step.wait(act, n, 4 * h + 4)
                        for c in range(3):
                            ins = act.activation(sig_of(h % 2)[:, c], acc[h % 2][:, c], ACT.Sigmoid)
                        sig_done.rise(ins)
                        if h >= 1:
                            copy_dots(h - 1)
                    copy_dots(H - 1)
                    for b in range(2):
                        dots_out[b].wait(act, n, H)
                        high_part[b].rise(act.copy(near_r[:, b], near[:, b]))

                    def copy_decays(b, m, j):
                        if j == 1 and m < NC - 1:
                            if m > 1:
                                past_decayed[b].wait(act, n, 4 * (m - 1))
                            t1 = (m + 1) * CH
                            since_copied[b].rise(act.copy(since[:, b, (m + 1) % 2, :, 1:CH + 1], decay[:, b, :, t1:t1 + CH]))

                    def boundary(b, m, part):
                        e = (2 * m + b) * 4
                        if part == 0:
                            t0 = m * CH
                            decayed[b].wait(act, n, (m + 1) * (CH - 1))
                            u_done[b].wait(act, n, t0 + CH)
                            joined[b].rise(act.copy(past[:, b, :, t0:t0 + CH], live[:, b, 0].rearrange("p i h -> p h i")))
                        for kind, q, i in pieces(part):
                            if kind == "turn" and i == 3:
                                past_turned.wait(act, n, e + q + 1)
                                if e + q >= 2:
                                    past_used.wait(act, n, e + q - 1)
                                past_out.rise(act.copy(pastT[0:(m + 1) * CH, q % 2], p_past[q % 2][0:(m + 1) * CH, :]
                                                       .rearrange("p (h v) -> p h v", h=4)))
                        if part == LAST_PART:
                            past_used.wait(act, n, e + 4)
                            if m > 0:
                                yk_done[b].wait(act, n, 2 * m)
                                yq_done[b].wait(act, n, m)
                            y0_out[b].rise(act.copy(y0[:, b, :, :], p_y0[b][:, :].rearrange("p (h c) -> p h c", h=H)))

                    for _, steps, parts in slots():
                        for x in steps:
                            copy_decays(*x)
                        for x in parts:
                            boundary(*x)

                    def square_of(i):
                        b, q = divmod(i, 4)
                        centred.wait(act, n, i + 1)
                        if i >= 2:
                            var_psum.wait(act, n, i - 1)
                        squared.rise(act.activation(square[i % 2], vb[:, b, 4 * q:4 * q + 4, :], ACT.Square))

                    def root_of(i):
                        var_psum.wait(act, n, i + 1)
                        if i >= 2:
                            normal.wait(act, n, i - 1)
                        rooted.rise(act.activation(root[i % 2], p_var[i % 2][:, :].rearrange("p (h t) -> p h t", t=T), ACT.Sqrt,
                                                   bias=g.eps[:, 0:1], scale=1.0 / HD))

                    square_of(0)
                    for i in range(8):
                        if i + 1 < 8:
                            square_of(i + 1)
                        root_of(i)

            @block.tensor
            def _(pe):
                projected.open(pe)
                pe.wait_ge(set_up, 10)
                with pe.Fori(0, TURNS) as n:

                    def project(h):
                        p = h % 2
                        w_loaded[p].wait(pe, n, h // 2 + 1)
                        gates_done.wait(pe, n, h - 1)
                        w = wbuf[p][:, 0:W_COLS].rearrange("p (c f) -> p c f", c=KT)
                        for i in range(6):
                            o = p_proj[p][i // 2][:, (i % 2) * N2:(i % 2 + 1) * N2]
                            for c in range(KT):
                                lhsT = w[:, c, i * P:(i + 1) * P] if i < 5 else w[:, c, 640:641].broadcast_to([P, P])
                                ins = pe.matmul(o, lhsT, xnT[:, c, :], start=(c == 0), stop=(c == KT - 1))
                        projected.rise(ins)

                    def dot(h):
                        p = h % 2
                        qkv_done.wait(pe, n, h + 1)
                        for b in range(2):
                            dots_out[b].wait(pe, n, h)
                            k, q, kb = k_h[p][:, b, :], q_h[p][:, b, :], kb_h[p][:, b, :]
                            for i in range(T // ROWS):
                                r, p0 = i * ROWS, i % 2 * 2 * ROWS
                                for kind, lhsT in ((KIND_K, kb[:, r + 1:r + ROWS + 1]), (KIND_Q, q[:, r:r + ROWS])):
                                    o = (2 * kind + i // 2) * ROWS
                                    for p1 in (p0, p0 + ROWS):
                                        pe.matmul(p_dots[b][p1:p1 + ROWS, o:o + ROWS], lhsT, k[:, r:r + ROWS], start=True, stop=True)
                            for kind, rhs in ((KIND_K, kb[:, 0:T]), (KIND_Q, q)):
                                ins = pe.matmul(p_dots[b][:, BANK // 2 + kind * T:BANK // 2 + (kind + 1) * T], k, rhs, start=True, stop=True)
                            dotted[b].rise(ins)

                    def spread_rows(b, m, j):
                        if j == 0:
                            return
                        e = m * CH + j
                        if e == 1:
                            split[b].wait(pe, n, 1)
                        if e > 2:
                            multiplied[b].wait(pe, n, e - 2)
                        block, row = divmod(m * CH + j - 1, ROWS)
                        i0 = m * CH % ROWS
                        first = 0 if j < CH else 1
                        spread[b].rise(pe.matmul(p_spread[b][j % 2][:, first * H * j:2 * H * j],
                                                 pair[:, block % 2, row:row + 1].broadcast_to([P, P]),
                                                 near_r[:, b, first:, block // 2, i0:i0 + j, :], start=True, stop=True))

                    def boundary(b, m, part):
                        e = (2 * m + b) * 4
                        k = (m + 1) * CH
                        if part == 0:
                            joined[b].wait(pe, n, m + 1)
                        for kind, q, i in pieces(part):
                            h = 4 * q + i
                            if kind == "turn":
                                if i == 0 and m > 0:
                                    past_decayed[b].wait(pe, n, 4 * (m - 1) + q + 1)
                                if i == 0 and e + q >= 2:
                                    past_out.wait(pe, n, e + q - 1)
                                ins = pe.transpose(p_past[q % 2][:, i * P:(i + 1) * P], past[:, b, h, :], g.ident[:, :])
                            else:
                                if i == 0:
                                    past_out.wait(pe, n, e + q + 1)
                                ins = pe.matmul(p_y0[b][:, h * 2 * CH:(h + 1) * 2 * CH], pastT[0:k, q % 2, i, :],
                                                dots[0:k, b, h, :, k:k + CH], start=True, stop=True)
                            if i == 3:
                                (past_turned if kind == "turn" else past_used).rise(ins)

                    normed.wait(pe, n, 2)
                    for b in range(2):
                        for c in range(KT):
                            o = c * N2 + b * T
                            ins = pe.transpose(g.banks[6][:, o:o + T], xn[:, b, c * P:(c + 1) * P], g.ident[:, :])
                    xnT_psum.rise(ins)
                    xnT_done.wait(pe, n, 1)
                    project(0)
                    project(1)
                    for h in range(H):
                        if h + 2 < H:
                            project(h + 2)
                        dot(h)

                    all_slots = list(slots())
                    for i, (_, steps, parts) in enumerate(all_slots):
                        if i == 0:
                            for x in steps:
                                spread_rows(*x)
                        if i + 1 < len(all_slots):
                            for x in all_slots[i + 1][1]:
                                spread_rows(*x)
                        for x in parts:
                            boundary(*x)

                    def mean_of(i):
                        b, q = divmod(i, 4)
                        if i == 0:
                            for x in range(2):
                                multiplied[x].wait(pe, n, NC * CH)
                        if i % 4 == 0:
                            o_done[b].wait(pe, n, NC)
                        if i >= 2:
                            centred.wait(pe, n, i - 1)
                        mean_psum.rise(pe.matmul(p_mean[i % 2][:, :], g.ones[:, :], vb[:, b, 4 * q:4 * q + 4, :], start=True, stop=True))

                    def var_of(i):
                        squared.wait(pe, n, i + 1)
                        if i >= 2:
                            rooted.wait(pe, n, i - 1)
                        var_psum.rise(pe.matmul(p_var[i % 2][:, :], g.ones[:, :], square[i % 2], start=True, stop=True))

                    mean_of(0)
                    mean_of(1)
                    for i in range(8):
                        if i + 2 < 8:
                            mean_of(i + 2)
                        var_of(i)
                    wo_loaded.wait(pe, n, 1)
                    for b in range(2):
                        for h in range(H):
                            if h % 4 == 0:
                                gated.wait(pe, n, 4 * b + h // 4 + 1)
                            ins = pe.matmul(p_out[b][:, 0:D], vb[:, b, h, :], wo[:, h, :], start=(h == 0), stop=(h == H - 1))
                        out_psum.rise(ins)
        s.close()


def layer0_cross(nc, g):
    norm_stats(nc, g, "n1")
    HEADS, HD, S = 16, 8, D
    PER_BLOCK = 4
    BIG = 1.0e6
    UNITS = [(tt, j, hp) for tt in range(2) for j in range(4) for hp in range(2)]
    NU = len(UNITS)
    scale = float(HD) ** -0.5
    with ExitStack() as st:
        s = Section(nc, st, "c0")
        wq, wk, wv = (s.sb(k, [P, P]) for k in ("wq", "wk", "wv"))
        bias_rows = s.sb("bias_rows", [1, 3 * P])
        head_rows = s.sb("head_rows", [P, PER_BLOCK])
        mask_all = s.sb("mask_all", [P, B, S])
        mask_col = s.sb("mask_col", [P, 2, B])
        mask_big = s.sb("mask_big", [P, 2, B])
        minus_big = s.sb("minus_big", [P, 1])
        pause = s.sb("pause", [P, 2])
        xn = s.sb("xn", [P, D])
        ctx_n = s.sb("ctx_n", [P, 2, D])
        qT = s.sb("qT", [P, D])
        kT = s.sb("kT", [P, S])
        k_spread = s.sb("k_spread", [P, PER_BLOCK, S])
        v_one = s.sb("v_one", [P, 2, HEADS, HD + 1])
        add_mask = s.sb("add_mask", [P, 2, S])
        probs = s.sb("probs", [P, 3, 2, S])
        low = s.sb("low", [P, 3, 2])
        probsT = s.sb("probsT", [P, 2, 2, 2, T])
        recip = s.sb("recip", [P, 2, HEADS])
        y = s.sb("y", [P, 2, P])
        loaded, ctx_loaded = s.sem("loaded"), [s.sem("ctx_loaded0"), s.sem("ctx_loaded1")]
        ctx_used = s.sem("ctx_used")
        ones_set, big_made, add_made = s.sem("ones_set"), s.sem("big_made"), s.sem("add_made")
        normed, projected, q_done, k_masked, k_done = (s.sem(k) for k in ("normed", "projected", "q_done", "k_masked", "k_done"))
        v_done, scored, negated, expd = (s.sem(k) for k in ("v_done", "scored", "negated", "expd"))
        turned, turned_out, weighed = (s.sem(k) for k in ("turned", "turned_out", "weighed"))
        recip_step, y_done, y_turned, added = (s.sem(k) for k in ("recip_step", "y_done", "y_turned", "added"))
        p_qk, p_v, p_av = g.banks[0], g.banks[1], g.banks[2]
        p_scores, p_turned = [g.banks[3], g.banks[4], g.banks[5]], [g.banks[6], g.banks[7]]
        av = p_av[:, 0:2 * HEADS * (HD + 1)].rearrange("p (t h e) -> p t h e", t=2, e=HD + 1)
        LOADS = 16 * 7

        with nc.Block() as block:

            @block.sync
            def _(sp):
                for dst, src in ((wq, "c0_wq"), (wk, "c0_wk"), (wv, "c0_wv"), (bias_rows, "c0_bias"),
                                 (head_rows, "head_rows8"), (mask_col, "c0_mask_col")):
                    sp.dma_start(dst[:], g.dram[src]).then_inc(loaded, 16)
                sp.dma_start(mask_all[:], g.dram["c0_mask"].partition_broadcast(P)).then_inc(loaded, 16)
                with sp.Fori(0, B // 2) as i:
                    for b in range(2):
                        sp.wait_ge(ctx_used, 2 * i + b + 1)
                        sp.dma_start(ctx_n[:, b, :], g.dram["ctx_2048"][bass.ds(2 * i + b, 1), :, :])\
                          .then_inc(ctx_loaded[b], 16)
                for b in range(2):
                    sp.wait_ge(ctx_loaded[b], 16 * B // 2)

            @block.vector
            def _(dve):
                def copy_out(n, u):
                    dve.wait_ge(turned, n * NU + u + 1)
                    if u >= 2:
                        dve.wait_ge(weighed, n * NU + u - 1)
                    dve.tensor_copy(probsT[:, u % 2], p_turned[u % 2][:, :].rearrange("p (h c t) -> p h c t", h=2, c=2))\
                       .then_inc(turned_out, 1)

                dve.sem_inc(added, 1)
                dve.memset(v_one[:, :, :, HD:HD + 1], 1.0).then_inc(ones_set, 1)
                dve.memset(minus_big[:, :], -BIG).then_inc(ones_set, 1)
                dve.wait_ge(loaded, LOADS)
                dve.tensor_scalar(mask_big[:, :, :], mask_col[:, :, :], BIG, None, ALU.mult).then_inc(big_made, 1)
                with dve.Fori(0, B // 2) as i:
                    for b in range(2):
                        n = 2 * i + b
                        dve.wait_ge(added, n + 1)
                        normalize(dve, g, xn[:, :], n).then_inc(normed, 1)
                        dve.wait_ge(projected, 2 * n + 1)
                        dve.scalar_tensor_tensor(qT[:, :], p_qk[:, 0:D], scale, mask_all[:, bass.ds(n, 1), :], ALU.mult,
                                                 ALU.mult).then_inc(q_done, 1)
                        dve.tensor_tensor(kT[:, :], p_qk[:, D:2 * D], mask_all[:, bass.ds(n, 1), :], ALU.mult).then_inc(k_masked, 1)
                        dve.wait_ge(k_masked, n + 1)
                        dve.tensor_tensor(k_spread[:, :, :], bcast(kT[:, :], 1, PER_BLOCK), bcast(head_rows[:, :], 2, S),
                                          ALU.mult).then_inc(k_done, 1)
                        for u, (tt, j, hp) in enumerate(UNITS):
                            dve.wait_ge(scored, n * NU + u + 1)
                            if u == 0:
                                dve.wait_ge(add_made, n + 1)
                            if u >= 2:
                                copy_out(n, u - 2)
                            else:
                                dve.memset(pause[:, u:u + 1], 0.0)
                            for h in range(2):
                                ins = dve.tensor_tensor_reduce(
                                    probs[:, u % 3, h], p_scores[u % 3][:, h * S:(h + 1) * S], add_mask[:, tt, :],
                                    -1.0, 3.0e38, ALU.add, ALU.min, low[:, u % 3, h:h + 1])
                            ins.then_inc(negated, 1)
                        copy_out(n, NU - 2)
                        copy_out(n, NU - 1)
                        dve.wait_ge(weighed, n * NU + NU)
                        dve.reciprocal(recip[:, :, :], av[:, :, :, HD]).then_inc(recip_step, 1)
                        dve.wait_ge(recip_step, 2 * n + 1)
                        dve.tensor_tensor(recip[:, :, :], recip[:, :, :],
                                          bcast(mask_col[:, :, bass.ds(n, 1)].rearrange("p t n -> p (t n)"), 2, HEADS),
                                          ALU.mult).then_inc(recip_step, 1)
                        dve.wait_ge(recip_step, 2 * n + 2)
                        for tt in range(2):
                            ins = dve.tensor_tensor(y[:, tt, :].rearrange("p (h e) -> p h e", e=HD), av[:, tt, :, 0:HD],
                                                    bcast(recip[:, tt, :], 2, HD), ALU.mult)
                        ins.then_inc(y_done, 1)
                        dve.wait_ge(y_turned, n + 1)
                        dve.tensor_tensor(g.x[:, bass.ds(n, 1), :], g.x[:, bass.ds(n, 1), :], p_v[:, 0:D], ALU.add)\
                           .then_inc(added, 1)

            @block.scalar
            def _(act):
                act.wait_ge(ones_set, 2)
                act.wait_ge(big_made, 1)
                act.wait_ge(loaded, LOADS)
                with act.Fori(0, B) as n:
                    act.wait_ge(normed, n + 1)
                    for tt in range(2):
                        ins = act.activation(add_mask[:, tt, :], mask_all[:, bass.ds(n, 1), :], ACT.Identity,
                                             bias=minus_big[:, :], scale=mask_big[:, tt, bass.ds(n, 1)])
                    ins.then_inc(add_made, 1)
                    act.wait_ge(projected, 2 * n + 2)
                    for c in range(2):
                        ins = act.activation(v_one[:, c, :, 0:HD], p_v[:, c * P:(c + 1) * P].rearrange("p (h e) -> p h e", e=HD),
                                             ACT.Copy, scale=mask_col[:, c, bass.ds(n, 1)])
                    ins.then_inc(v_done, 1)
                    for u in range(NU):
                        act.wait_ge(negated, n * NU + u + 1)
                        for h in range(2):
                            ins = act.activation(probs[:, u % 3, h], probs[:, u % 3, h], ACT.Exp,
                                                 bias=low[:, u % 3, h:h + 1], scale=-1.0)
                        ins.then_inc(expd, 1)

            @block.tensor
            def _(pe):
                pe.sem_inc(ctx_used, 2)
                pe.wait_ge(loaded, LOADS)
                with pe.Fori(0, B // 2) as i:
                    for b in range(2):
                        n = 2 * i + b
                        pe.wait_ge(normed, n + 1)
                        pe.matmul(p_qk[:, 0:D], wq[:, :], xn[:, :], start=True, stop=False)
                        pe.matmul(p_qk[:, 0:D], bias_rows[0:1, 0:P], bcast(g.ones[0:1, 0:P], 1, 2), start=False, stop=True)
                        pe.wait_ge(ctx_loaded[b], 16 * i + 16)
                        pe.matmul(p_qk[:, D:2 * D], wk[:, :], ctx_n[:, b, :], start=True, stop=False)
                        pe.matmul(p_qk[:, D:2 * D], bias_rows[0:1, P:2 * P], bcast(g.ones[0:1, 0:P], 1, 2),
                                  start=False, stop=True).then_inc(projected, 1)
                        for c in range(2):
                            o = p_v[:, c * P:(c + 1) * P]
                            ins = pe.matmul(o, ctx_n[:, b, c * P:(c + 1) * P], wv[:, :], start=True, stop=False)
                            ins2 = pe.matmul(o, g.ones[0:1, 0:P], bias_rows[0:1, 2 * P:3 * P], start=False, stop=True)
                        ins.then_inc(ctx_used, 1)
                        ins2.then_inc(projected, 1)

                        def scores(u):
                            tt, j, hp = UNITS[u]
                            if u == 0:
                                pe.wait_ge(q_done, n + 1)
                                pe.wait_ge(k_done, n + 1)
                            if u >= 3:
                                pe.wait_ge(negated, n * NU + u - 2)
                            rows = slice(32 * j, 32 * j + 32)
                            pe.matmul(p_scores[u % 3][:, :], qT[rows, tt * P:(tt + 1) * P], k_spread[rows, 2 * hp:2 * hp + 2, :],
                                      start=True, stop=True).then_inc(scored, 1)

                        def turn(u):
                            pe.wait_ge(expd, n * NU + u + 1)
                            if u >= 2:
                                pe.wait_ge(turned_out, n * NU + u - 1)
                            for h in range(2):
                                for c in range(2):
                                    o = (2 * h + c) * T
                                    ins = pe.transpose(p_turned[u % 2][:, o:o + T], probs[:, u % 3, h, c * P:(c + 1) * P], g.ident[:, :])
                            ins.then_inc(turned, 1)

                        def weigh(u):
                            tt, j, hp = UNITS[u]
                            if u == 0:
                                pe.wait_ge(v_done, n + 1)
                            pe.wait_ge(turned_out, n * NU + u + 1)
                            for h in range(2):
                                head = PER_BLOCK * j + 2 * hp + h
                                for c in range(2):
                                    ins = pe.matmul(av[:, tt, head, :], probsT[:, u % 2, h, c, :], v_one[:, c, head, :],
                                                    start=(c == 0), stop=(c == 1))
                            ins.then_inc(weighed, 1)

                        scores(0)
                        scores(1)
                        turn(0)
                        for u in range(1, NU):
                            if u + 1 < NU:
                                scores(u + 1)
                            turn(u)
                            weigh(u - 1)
                        weigh(NU - 1)
                        pe.wait_ge(y_done, n + 1)
                        for tt in range(2):
                            ins = pe.transpose(p_v[:, tt * P:(tt + 1) * P], y[:, tt, :], g.ident[:, :])
                        ins.then_inc(y_turned, 1)
        s.close()


def gated_mlp(nc, s, g, tiles, act_fn, strided, wg, wu, wd, router):
    n_tok = 2 * T
    turns = B // 2
    xn = s.sb("xn", [P, 2, D])
    xnT = s.sb("xnT", [P, KT, n_tok])
    gated = s.sb("gated", [P, 2, n_tok])
    hidden = s.sb("hidden", [P, 3, n_tok])
    normed, xnT_psum, xnT_done = s.sem("normed"), s.sem("xnT_psum"), s.sem("xnT_done")
    projected, activated, upped = s.sem("projected"), s.sem("activated"), s.sem("upped")
    hidden_done, downed, added = s.sem("hidden_done"), s.sem("downed"), s.sem("added")
    p_turn, p_gu = g.banks[0], [g.banks[1], g.banks[2], g.banks[3]]
    p_weight, p_acc, p_route = [g.banks[4], g.banks[7]], [g.banks[5], g.banks[6]], g.banks[0]
    if router:
        NE = router["experts"] + 1
        wr, expert_rows = router["wr"], router["expert_rows"]
        raw = s.sb("raw", [P, 2, NE])
        top8 = s.sb("top8", [P, 2, 8])
        rest = s.sb("rest", [P, 2, NE - 1])
        stat = s.sb("stat", [P, 4, 2])
        shared_tanh = s.sb("shared_tanh", [P, 2, 1])
        mix = s.sb("mix", [P, 2, NE])
        pause = s.sb("pause", [P, 1])
        combT = s.sb("combT", [NE, n_tok])
        weighted = s.sem("weighted")
        routed_in, route_step = s.sem("routed_in"), s.sem("route_step")
        exp_done, mix_done = s.sem("exp_done"), s.sem("mix_done")
        mix_turned, combT_done = s.sem("mix_turned"), s.sem("combT_done")
        ROUTE_STEPS = 14

    with nc.Block() as block:

        @block.vector
        def _(dve):
            dve.sem_inc(added, 2)
            if router:
                step = Steps(dve, route_step, ROUTE_STEPS)
            with dve.Fori(0, turns) as n:
                dve.wait_ge(added, 2 * n + 2)
                for b in range(2):
                    normalize(dve, g, xn[:, b, :], 2 * n + b).then_inc(normed, 1)
                if router:
                    step.turn(n)
                    dve.wait_ge(routed_in, n + 1)
                    logits = p_route[:, 0:2 * NE].rearrange("p (b e) -> p b e", e=NE)
                    step.did(dve.tensor_reduce(stat[:, 0], logits[:, :, 0:NE - 1], AX, ALU.max))
                    step.wait()
                    step.did(dve.tensor_tensor(raw[:, :, 0:NE - 1], logits[:, :, 0:NE - 1], bcast(stat[:, 0], 2, NE - 1), ALU.subtract))
                    dve.wait_ge(exp_done, n + 1)
                    step.did(dve.tensor_reduce(stat[:, 1], raw[:, :, 0:NE - 1], AX, ALU.add))
                    step.wait()
                    step.did(dve.reciprocal(stat[:, 1], stat[:, 1]))
                    step.wait()
                    step.did(dve.tensor_tensor(raw[:, :, 0:NE - 1], raw[:, :, 0:NE - 1], bcast(stat[:, 1], 2, NE - 1), ALU.mult))
                    step.wait()
                    dve.memset(pause[:, :], 0.0)
                    for b in range(2):
                        ins = dve.max(top8[:, b, :], raw[:, b, 0:NE - 1])
                    step.did(ins)
                    step.wait()
                    step.did(dve.memset(top8[:, :, router["top"]:], -1.0))
                    step.wait()
                    dve.memset(pause[:, :], 0.0)
                    for b in range(2):
                        ins = dve.match_replace(rest[:, b, :], top8[:, b, :], raw[:, b, 0:NE - 1], 0.0)
                    step.did(ins)
                    step.wait()
                    step.did(dve.tensor_tensor(mix[:, :, 0:NE - 1], raw[:, :, 0:NE - 1], rest[:, :, :], ALU.subtract))
                    step.wait()
                    step.did(dve.tensor_reduce(stat[:, 2], mix[:, :, 0:NE - 1], AX, ALU.add))
                    step.wait()
                    step.did(dve.tensor_scalar(stat[:, 2], stat[:, 2], 1e-9, None, ALU.max))
                    step.wait()
                    step.did(dve.reciprocal(stat[:, 3], stat[:, 2]))
                    step.wait()
                    step.did(dve.tensor_tensor(mix[:, :, 0:NE - 1], mix[:, :, 0:NE - 1], bcast(stat[:, 3], 2, NE - 1), ALU.mult))
                    step.did(dve.tensor_scalar(mix[:, :, NE - 1:NE], shared_tanh[:, :, :], 0.5, 0.5, ALU.mult, ALU.add))
                    step.end()
                for t in range(tiles):
                    dve.wait_ge(activated, n * tiles + t + 1)
                    if t >= 3:
                        dve.wait_ge(downed, n * tiles + t - 2)
                    up = p_gu[t % 3][:, n_tok:2 * n_tok]
                    if not router:
                        dve.tensor_tensor(hidden[:, t % 3, :], gated[:, t % 2, :], up, ALU.mult).then_inc(hidden_done, 1)
                        continue
                    dve.tensor_tensor(gated[:, t % 2, :], gated[:, t % 2, :], up, ALU.mult).then_inc(upped, 1)
                    dve.wait_ge(upped, n * tiles + t + 1)
                    dve.wait_ge(weighted, n * tiles + t + 1)
                    dve.tensor_tensor(hidden[:, t % 3, :], gated[:, t % 2, :], p_weight[t % 2][:, 0:n_tok], ALU.mult)\
                       .then_inc(hidden_done, 1)
                dve.wait_ge(downed, n * tiles + tiles)
                for b in range(2):
                    dve.tensor_tensor(g.x[:, bass.ds(2 * n + b, 1), :], g.x[:, bass.ds(2 * n + b, 1), :],
                                      p_acc[b][:, 0:D], ALU.add).then_inc(added, 1)

        @block.scalar
        def _(act):
            with act.Fori(0, turns) as n:
                act.wait_ge(xnT_psum, n + 1)
                act.copy(xnT[:, :, :], p_turn[:, :].rearrange("p (c t) -> p c t", c=KT)).then_inc(xnT_done, 1)
                if router:
                    logits = p_route[:, 0:2 * NE].rearrange("p (b e) -> p b e", e=NE)
                    act.wait_ge(route_step, n * ROUTE_STEPS + 2)
                    act.activation(shared_tanh[:, :, :], logits[:, :, NE - 1:NE], ACT.Tanh, scale=0.5)
                    act.activation(raw[:, :, 0:NE - 1], raw[:, :, 0:NE - 1], ACT.Exp).then_inc(exp_done, 1)
                    act.wait_ge(mix_turned, n + 1)
                    act.copy(combT[:, :], p_route[0:NE, n_tok:2 * n_tok]).then_inc(combT_done, 1)
                for t in range(tiles):
                    act.wait_ge(projected, n * tiles + t + 1)
                    if t >= 2:
                        act.wait_ge(hidden_done, n * tiles + t - 1)
                    act.activation(gated[:, t % 2, :], p_gu[t % 3][:, 0:n_tok], act_fn).then_inc(activated, 1)

        @block.tensor
        def _(pe):
            with pe.Fori(0, turns) as n:
                pe.wait_ge(normed, 2 * n + 2)
                for b in range(2):
                    for c in range(KT):
                        src = xn[:, b, c::2] if strided else xn[:, b, c * P:(c + 1) * P]
                        o = c * n_tok + b * T
                        ins = pe.transpose(p_turn[:, o:o + T], src, g.ident[:, :])
                ins.then_inc(xnT_psum, 1)
                pe.wait_ge(xnT_done, n + 1)
                if router:
                    for b in range(2):
                        for c in range(KT):
                            ins = pe.matmul(p_route[:, b * NE:(b + 1) * NE], xnT[:, c, b * T:(b + 1) * T], wr[:, c, :],
                                            start=(c == 0), stop=(c == KT - 1))
                    ins.then_inc(routed_in, 1)

                def up(t):
                    if t >= 3:
                        pe.wait_ge(hidden_done, n * tiles + t - 2)
                    for w, o in ((wg, 0), (wu, n_tok)):
                        for c in range(KT):
                            ins = pe.matmul(p_gu[t % 3][:, o:o + n_tok], w[:, c, t * P:(t + 1) * P], xnT[:, c, :],
                                            start=(c == 0), stop=(c == KT - 1))
                    ins.then_inc(projected, 1)

                def weight(t):
                    if t >= 2:
                        pe.wait_ge(hidden_done, n * tiles + t - 1)
                    pe.matmul(p_weight[t % 2][:, 0:n_tok], expert_rows[:, t * P:(t + 1) * P], combT[:, :],
                              start=True, stop=True).then_inc(weighted, 1)

                def down(t):
                    pe.wait_ge(hidden_done, n * tiles + t + 1)
                    for b in range(2):
                        ins = pe.matmul(p_acc[b][:, 0:D], hidden[:, t % 3, b * T:(b + 1) * T], wd[:, t, :],
                                        start=(t == 0), stop=(t == tiles - 1))
                    ins.then_inc(downed, 1)

                up(0)
                up(1)
                if router:
                    pe.wait_ge(route_step, (n + 1) * ROUTE_STEPS)
                    for b in range(2):
                        o = n_tok + b * T
                        ins = pe.transpose(p_route[0:NE, o:o + T], mix[:, b, :], g.ident[:, :])
                    ins.then_inc(mix_turned, 1)
                    pe.wait_ge(combT_done, n + 1)
                    weight(0)
                for t in range(1, tiles):
                    if t + 1 < tiles:
                        up(t + 1)
                    if router:
                        weight(t)
                    down(t - 1)
                down(tiles - 1)


def layer1_moe(nc, g):
    norm_stats(nc, g, "n5")
    tiles = g.dram["e1_wg"].shape[-1] // P
    with ExitStack() as st:
        s = Section(nc, st, "e1")
        wg = s.sb("wg", [P, KT, tiles * P])
        wu = s.sb("wu", [P, KT, tiles * P])
        wd = s.sb("wd", [P, tiles, D])
        wr = s.sb("wr", [P, KT, 17])
        expert_rows = s.sb("expert_rows", [17, tiles * P])
        loaded = s.sem("loaded")
        with nc.Block() as block:

            @block.sync
            def _(sp):
                for dst, src in ((wr, "wr"), (wg, "wg"), (wu, "wu"), (wd, "wd"), (expert_rows, "expert_rows")):
                    sp.dma_start(dst[:], g.dram["e1_" + src]).then_inc(loaded, 16)
                sp.wait_ge(loaded, 16 * 5)

        gated_mlp(nc, s, g, tiles, ACT.Silu, False, wg, wu, wd,
                  dict(experts=16, top=4, wr=wr, expert_rows=expert_rows))
        s.close()


def layer0_mlp(nc, g):
    norm_stats(nc, g, "n2")
    F = 2048
    CH = 1024
    with ExitStack() as st:
        s = Section(nc, st, "m0")
        wg = s.sb("wg", [P, KT, F])
        wu = s.sb("wu", [P, KT, F])
        wd = s.sb("wd", [P, F // P, D])
        with ExitStack() as st2:
            q = Section(nc, st2, "m0q")
            codes = q.sb("codes", [P, 3, F], I32)
            scales = q.sb("scales", [P, 3, F])
            m = q.sb("m", [P, 2, CH], I32)
            sign = q.sb("sign", [P, 2, CH], I32)
            over4 = q.sb("over4", [P, 2, CH])
            over6 = q.sb("over6", [P, 2, CH])
            signed_scale = q.sb("signed_scale", [P, 2, CH])
            bias = q.sb("bias", [P, 3])
            loaded, bias_set = [q.sem(f"loaded{k}") for k in range(3)], q.sem("bias_set")
            bits, sloped, sign_done = q.sem("bits"), q.sem("sloped"), q.sem("sign_done")
            scaled, summed, valued, done = q.sem("scaled"), q.sem("summed"), q.sem("valued"), q.sem("done")
            dests = []
            for k in range(3):
                for half in range(F // CH):
                    for par in range(2):
                        cols = slice(half * CH, (half + 1) * CH)
                        if k < 2:
                            out = (wg, wu)[k][:, par, cols]
                        else:
                            per = CH // D
                            out = wd[:, :, :].rearrange("p (j r) d -> p j r d", r=2)[:, half * per:(half + 1) * per, par, :]
                        dests.append((out, k, par, cols))
            with nc.Block() as block:

                @block.sync
                def _(sp):
                    for k in range(3):
                        sp.dma_start(codes[:, k, :], g.dram["m0_codes"][:, k, :]).then_inc(loaded[k], 16)
                        for r in range(8):
                            sp.dma_start(scales[16 * r:16 * r + 16, k, :],
                                         g.dram["m0_scales"][r, k, :].partition_broadcast(16)).then_inc(loaded[k], 16)

                @block.vector
                def _(dve):
                    dve.memset(bias[:, 0:1], -2.0).then_inc(bias_set, 1)
                    dve.memset(bias[:, 1:2], -6.0).then_inc(bias_set, 1)
                    dve.memset(bias[:, 2:3], 1.0).then_inc(bias_set, 1)

                    def split(i):
                        out, k, par, cols = dests[i]
                        dve.wait_ge(loaded[k], 144)
                        if i >= 2:
                            dve.wait_ge(valued, i - 1)
                            dve.wait_ge(sloped, 3 * (i - 1))
                        dve.tensor_scalar(m[:, i % 2], codes[:, k, cols], 4 * par, 7, ALU.logical_shift_right, ALU.bitwise_and)
                        dve.tensor_scalar(sign[:, i % 2], codes[:, k, cols], 4 * par + 3, 1, ALU.logical_shift_right,
                                          ALU.bitwise_and).then_inc(bits, 1)

                    def combine(i):
                        out, k, par, cols = dests[i]
                        dve.wait_ge(sloped, 3 * (i + 1))
                        dve.tensor_tensor(over4[:, i % 2], over4[:, i % 2], over6[:, i % 2], ALU.add).then_inc(summed, 1)
                        dve.wait_ge(summed, i + 1)
                        dve.scalar_tensor_tensor(over6[:, i % 2], m[:, i % 2], 0.5, over4[:, i % 2], ALU.mult, ALU.add)\
                           .then_inc(valued, 1)
                        dve.wait_ge(valued, i + 1)
                        dve.wait_ge(scaled, i + 1)
                        ss, v = signed_scale[:, i % 2], over6[:, i % 2]
                        if k == 2:
                            ss, v = (a.rearrange("p (j d) -> p j d", d=D) for a in (ss, v))
                        dve.tensor_tensor(out, v, ss, ALU.mult).then_inc(done, 1)

                    split(0)
                    for i in range(len(dests)):
                        if i + 1 < len(dests):
                            split(i + 1)
                        combine(i)
                    dve.wait_ge(done, len(dests))

                @block.scalar
                def _(act):
                    act.wait_ge(bias_set, 3)
                    for i in range(len(dests)):
                        act.wait_ge(bits, i + 1)
                        if i >= 2:
                            act.wait_ge(done, i - 1)
                        act.activation(over4[:, i % 2], m[:, i % 2], ACT.Relu, bias=bias[:, 0:1], scale=0.5).then_inc(sloped, 1)
                        act.activation(over6[:, i % 2], m[:, i % 2], ACT.Relu, bias=bias[:, 1:2]).then_inc(sloped, 1)
                        act.activation(signed_scale[:, i % 2], sign[:, i % 2], ACT.Identity, bias=bias[:, 2:3], scale=-2.0)\
                           .then_inc(sloped, 1)

                @block.gpsimd
                def _(pool):
                    for i, (out, k, par, cols) in enumerate(dests):
                        pool.wait_ge(loaded[k], 144)
                        pool.wait_ge(sloped, 3 * (i + 1))
                        pool.tensor_tensor(signed_scale[:, i % 2], signed_scale[:, i % 2], scales[:, k, cols], ALU.mult)\
                            .then_inc(scaled, 1)
            q.close()

        gated_mlp(nc, s, g, F // P, ACT.Gelu_apprx_tanh, True, wg, wu, wd, None)
        s.close()


class Globals:
    pass


def build(nc, dram, out):
    g = Globals()
    g.dram = dram
    with ExitStack() as st:
        s = Section(nc, st, "g")
        g.x = s.sb("x", [P, B, D])
        g.mean_var = s.sb("mean_var", [P, B, 2])
        g.rstd = s.sb("rstd", [P, B])
        g.ident = s.sb("ident", [P, P])
        g.ones = s.sb("ones", [P, P])
        g.eps = s.sb("eps", [P, 1])
        g.banks = [st.enter_context(nc.psum_tensor(f"bank{i}", [P, BANK], F32)) for i in range(8)]
        x_loaded, constants_set, stored = s.sem("x_loaded"), s.sem("constants_set"), s.sem("stored")
        with nc.Block() as block:

            @block.sync
            def _(sp):
                sp.dma_start(g.x[:, :, :], dram["x"].rearrange("b t d -> t b d")).then_inc(x_loaded, 16)
                sp.dma_start(g.ident[:, :], dram["ident"]).then_inc(x_loaded, 16)
                sp.wait_ge(x_loaded, 32)

            @block.vector
            def _(dve):
                dve.memset(g.ones[:, :], 1.0).then_inc(constants_set, 1)
                dve.memset(g.eps[:, :], EPS).then_inc(constants_set, 1)
                dve.wait_ge(constants_set, 2)

        sublayers = (layer0_attention, layer0_cross, layer0_mlp, layer1_attention, layer1_cross, layer1_moe)
        for k in STAGES:
            sublayers[k](nc, g)

        with nc.Block() as block:

            @block.sync
            def _(sp):
                sp.dma_start(out.rearrange("b t d -> t b d"), g.x[:, :, :]).then_inc(stored, 16)
                sp.wait_ge(stored, 16)


def contraction_major(a):
    return np.ascontiguousarray(a.reshape(-1, P, a.shape[-1]).transpose(1, 0, 2))


def constants():
    c = {"ident": np.eye(P, dtype=np.float32)}
    c["causal"] = np.where(np.tril(np.ones((T, T), bool)), 0.0, MASKED).astype(np.float32)
    rows = np.arange(P)
    for hd in (8, 16):
        per_block = 32 // hd
        c[f"head_rows{hd}"] = ((rows[:, None] // hd) % per_block == np.arange(per_block)[None]).astype(np.float32)
    hd = 16
    theta = np.power(np.float32(10000.0), -np.float32(2.0) ** np.arange(hd // 2, dtype=np.float32) / np.float32(hd))
    angle = (np.arange(1, T + 1, dtype=np.float32)[None, :] * theta[:, None].astype(np.float32)).astype(np.float32)
    angle = np.tile(np.concatenate([angle, angle], 0), (P // hd, 1))
    sign = np.where((rows % hd) < hd // 2, -1.0, 1.0)[:, None]
    c["cos_sin"] = np.stack([np.cos(angle), np.sin(angle) * sign], 1).astype(np.float32)
    return c


def lay_out(i):
    f = {k: np.ascontiguousarray(v) for k, v in i.items()}
    d = {"x": f["x"], "mask_BxS2_if1": f["mask_BxS2_if1"]}
    ctx = f["ctx_2048"]
    d["ctxT"] = np.ascontiguousarray(ctx.transpose(2, 0, 1).reshape(KT, P, B, T).transpose(1, 0, 2, 3))
    wqkv, bqkv = f["L1_attn_Wqkv"], f["L1_attn_bqkv"]
    swap = (np.arange(D) // 16) * 16 + (np.arange(D) + 8) % 16
    for name, k in (("a1_wq", 0), ("a1_wk", 1)):
        m = wqkv[k * D:(k + 1) * D]
        d[name] = contraction_major(np.concatenate([m, m[swap]], 0).T)
    d["a1_wv"] = contraction_major(wqkv[2 * D:].T)
    d["a1_wo"] = contraction_major(f["L1_attn_Wo"].T)
    d["a1_bias"] = np.concatenate([bqkv[:D], bqkv[:D][swap], bqkv[D:2 * D], bqkv[D:2 * D][swap], bqkv[2 * D:],
                                   f["L1_attn_bo"]])[None]
    d["c1_wq"] = contraction_major(f["L1_xattn_w_q"].T)
    d["c1_wk"] = contraction_major(np.repeat(f["L1_xattn_w_k"].reshape(8, 1, 8, D), 4, axis=1).reshape(D, D).T)
    d["c1_wv"] = contraction_major(f["L1_xattn_w_v"].T)
    d["c1_wo"] = contraction_major(f["L1_xattn_w_o"].T)
    d["c1_bias"] = np.concatenate([np.zeros(3 * D, np.float32), f["L1_xattn_b_o"]])[None]
    H = 16
    per_head = [f[f"L0_attn_W{k}"].T.reshape(KT, P, H, P) for k in "qkvag"] + [f["L0_attn_Wb"].T.reshape(KT, P, H, 1)]
    cols = np.concatenate(per_head, -1).transpose(2, 1, 0, 3).reshape(H, P, KT * 641)
    taps = [f[f"L0_attn_conv_{k}_w"].reshape(H, P, 4) for k in "qkv"]
    rows = [f[f"L0_attn_conv_{k}_b"].reshape(H, P, 1) for k in "qkv"] + [f["L0_attn_ba"].reshape(H, P, 1)]
    bb = np.repeat(f["L0_attn_bb"].reshape(H, 1, 1), P, axis=1)
    d["a0_w"] = np.concatenate([cols, *taps, *rows, bb], -1)
    d["a0_wo"] = contraction_major(f["L0_attn_Wo"].T)
    d["a0_ln"] = np.stack([f["L0_attn_ln_g"], f["L0_attn_ln_b"]], 1)
    d["ctx_2048"] = ctx
    d["c0_wq"], d["c0_wk"], d["c0_wv"] = (np.ascontiguousarray(f[f"L0_xattn_W{k}"].T) for k in "qkv")
    d["c0_bias"] = np.concatenate([f["L0_xattn_bq"], f["L0_xattn_bk"], f["L0_xattn_bv"]])[None]
    d["c0_mask"] = f["mask_Bx1x2048_fk1"][:, 0]
    d["c0_mask_col"] = np.ascontiguousarray(f["mask_Bx1x2048_fk1"][:, 0].reshape(B, 2, P).transpose(2, 1, 0))
    hidden = 16 * 176 + 704
    fill = -hidden % P
    beside = lambda a: a.transpose(1, 0, 2).reshape(D, 16 * 176)
    pad_cols = np.zeros((D, fill), np.float32)
    d["e1_wg"] = contraction_major(np.concatenate([beside(f["L1_ffn_w_gate"]), f["L1_ffn_sh_gate"], pad_cols], 1))
    d["e1_wu"] = contraction_major(np.concatenate([beside(f["L1_ffn_w_up"]), f["L1_ffn_sh_up"], pad_cols], 1))
    d["e1_wd"] = contraction_major(np.concatenate([f["L1_ffn_w_down"].reshape(16 * 176, D), f["L1_ffn_sh_down"], pad_cols.T], 0))
    d["e1_wr"] = contraction_major(np.concatenate([f["L1_ffn_router_w"].T, f["L1_ffn_sh_gate_w"]], 1))
    expert = np.minimum(np.arange(hidden + fill) // 176, 16)
    d["e1_expert_rows"] = (expert[None, :] == np.arange(17)[:, None]).astype(np.float32)
    order = np.arange(2048).reshape(8, P, 2).transpose(0, 2, 1).ravel()
    down = f["L0_ffn_down_W_packed"].T.reshape(8, P, D).transpose(1, 0, 2).reshape(P, 2048)
    d["m0_codes"] = np.stack([f["L0_ffn_gate_W_packed"][order].T, f["L0_ffn_up_W_packed"][order].T, down], 1)
    down = f["L0_ffn_down_scales"].T.reshape(8, 8, D).transpose(1, 0, 2).reshape(8, 2048)
    d["m0_scales"] = np.stack([f["L0_ffn_gate_scales"][order].T, f["L0_ffn_up_scales"][order].T, down], 1)
    d.update(constants())
    return d


def kernel(**inputs):
    import concourse.bacc as bacc
    from concourse.bass_utils import run_bass_kernel_spmd as run

    nc = bacc.Bacc("TRN2", target_bir_lowering=False, num_devices=1)
    arrays = {f"in_{k}": np.ascontiguousarray(v) for k, v in lay_out(inputs).items()}
    dram = {k[3:]: nc.dram_tensor(k, v.shape, mybir.dt.from_np(v.dtype), kind="ExternalInput").ap()
            for k, v in arrays.items()}
    out = nc.dram_tensor("out", (B, T, D), F32, kind="ExternalOutput").ap()
    build(nc, dram, out)
    r = run(nc, [arrays], core_ids=[0])
    return r.results[0]["out"]
```
